# Optimizing a Trainium2 kernel written in Bass

```python
import numpy as np
import jax
import jax.numpy as jnp

def _softmax(x, axis=-1):
    return jax.nn.softmax(x, axis=axis)

def _gelu(x):
    return jax.nn.gelu(x, approximate=True)

def _silu(x):
    return jax.nn.silu(x)

def _sigmoid(x):
    return jax.nn.sigmoid(x)

def _layernorm(x, axis=-1, eps=1e-05):
    m = jnp.mean(x, axis=axis, keepdims=True)
    v = jnp.var(x, axis=axis, keepdims=True)
    return (x - m) / jnp.sqrt(v + eps)

def _scatter_add(tgt, idx, src, axis=0):
    return tgt.at[idx].add(src)

def _segment_sum(src, seg, n):
    return jax.ops.segment_sum(src, seg, n)
kernel_name = 'mk_xattn_ffn_d1_seqx_r4_d9d9d3'

def setup_inputs(seed: int=0):
    np.random.seed(seed)
    _w = jnp.asarray

    def _rec_inputs():
        import jax
        import jax.numpy as jnp
        _rk = jax.random.key(seed)
        x = 7.22e-05 + 1 * jax.random.normal(jax.random.fold_in(_rk, 1), (16, 256, 512), jnp.float32)
        _lenS = 256 - jax.random.randint(jax.random.fold_in(_rk, 7), (16,), 0, max(1, 256 // 4) + 1, jnp.int32)
        _lenS2 = 256 - jax.random.randint(jax.random.fold_in(_rk, 8), (16,), 0, max(1, 256 // 4) + 1, jnp.int32)
        _ctx_2048P = jax.random.normal(jax.random.fold_in(_rk, 11), (16, 16, 512), jnp.float32)
        _ctx_2048c = jax.random.dirichlet(jax.random.fold_in(_rk, 511), 0.3 * jnp.ones((16,), jnp.float32), (16, 256))
        _ctx_2048t = jnp.einsum('bsk,bkd->bsd', _ctx_2048c, _ctx_2048P)
        _ctx_2048t = _ctx_2048t * jax.lax.rsqrt(jnp.mean(jnp.square(_ctx_2048t)) + 1e-12) * 0.953939
        ctx_2048 = 4.13588e-05 + 0.999923 * (_ctx_2048t + 0.3 * jax.random.normal(jax.random.fold_in(_rk, 611), (16, 256, 512), jnp.float32))
        return (x, ctx_2048)
    x, ctx_2048 = _rec_inputs()

    def _L0_xattn_setup():
        import jax, jax.numpy as jnp
        import numpy as np
        BS, S, DK = (8, 128, 512)
        key = jax.random.key(seed)
        kq, kk, kv = jax.random.split(key, 3)
        q = jax.random.normal(kq, (BS, S, DK), dtype=jnp.float32)
        k = jax.random.normal(kk, (BS, S, DK), dtype=jnp.float32)
        v = jax.random.normal(kv, (BS, S, DK), dtype=jnp.float32)
        return {'q': q, 'k': k, 'v': v}
    _L0_xattn_all = _L0_xattn_setup()
    _L0_xattn_in = {k: v for k, v in _L0_xattn_all.items() if k in ()}
    del _L0_xattn_all

    def _L0_ffn_setup():
        import jax, jax.numpy as jnp
        import numpy as np
        _FP4_LUT = jnp.array([0.0, 0.5, 1.0, 1.5, 2.0, 3.0, 4.0, 6.0, -0.0, -0.5, -1.0, -1.5, -2.0, -3.0, -4.0, -6.0], dtype=jnp.float32)
        GROUP_SIZE = 128
        EPS = 1e-06

        def _dequant_fp4(packed_i32, scales_f16, group_size):
            out_f, in_p = packed_i32.shape
            w = packed_i32.astype(jnp.uint32)
            shifts = jnp.arange(8, dtype=jnp.uint32) * 4
            nib = w[:, :, None] >> shifts & jnp.uint32(15)
            vals = _FP4_LUT[nib.astype(jnp.int32)].reshape(out_f, in_p * 8)
            s = scales_f16.astype(jnp.float32).T
            s_full = jnp.repeat(s, group_size, axis=1)
            return vals * s_full
        key = jax.random.key(seed)
        k1, k2, k3, k4, k5 = jax.random.split(key, 5)
        B, S, H, I = (4, 512, 512, 1408)
        x = jax.random.normal(k1, (B, S, H), dtype=jnp.float32)
        gate_up_packed = jax.random.randint(k2, (2 * I, H // 8), 0, 2147483647, dtype=jnp.int32)
        gate_up_scales = jax.random.uniform(k3, (H // GROUP_SIZE, 2 * I), dtype=jnp.float32).astype(jnp.float16)
        down_packed = jax.random.randint(k4, (H, I // 8), 0, 2147483647, dtype=jnp.int32)
        down_scales = jax.random.uniform(k5, (I // GROUP_SIZE, H), dtype=jnp.float32).astype(jnp.float16)
        return {'x': x, 'gate_up_packed': gate_up_packed, 'gate_up_scales': gate_up_scales, 'down_packed': down_packed, 'down_scales': down_scales}
    _L0_ffn_all = _L0_ffn_setup()
    _L0_ffn_in = {k: v for k, v in _L0_ffn_all.items() if k in ('gate_up_packed', 'gate_up_scales', 'down_packed', 'down_scales')}
    del _L0_ffn_all
    return {'x': x, 'ctx_2048': ctx_2048, 'L0_ffn_gate_up_packed': _L0_ffn_in['gate_up_packed'], 'L0_ffn_gate_up_scales': _L0_ffn_in['gate_up_scales'], 'L0_ffn_down_packed': _L0_ffn_in['down_packed'], 'L0_ffn_down_scales': _L0_ffn_in['down_scales']}

def reference(x, ctx_2048, L0_ffn_gate_up_packed, L0_ffn_gate_up_scales, L0_ffn_down_packed, L0_ffn_down_scales):
    import jax
    import jax.numpy as jnp

    def _L0_xattn_ref(q, k, v):
        import jax, jax.numpy as jnp
        import numpy as np
        BS, S, DK = (8, 128, 512)
        dk = q.shape[-1]
        scale = 1.0 / jnp.sqrt(jnp.asarray(dk, dtype=q.dtype))
        scaled = jnp.einsum('bsd,bse->bde', q, k) * scale
        attn = jax.nn.softmax(scaled, axis=1)
        out = jnp.einsum('bde,bse->bsd', attn, v)
        return out

    def _L0_ffn_ref(x, gate_up_packed, gate_up_scales, down_packed, down_scales):
        import jax, jax.numpy as jnp
        import numpy as np
        _FP4_LUT = jnp.array([0.0, 0.5, 1.0, 1.5, 2.0, 3.0, 4.0, 6.0, -0.0, -0.5, -1.0, -1.5, -2.0, -3.0, -4.0, -6.0], dtype=jnp.float32)
        GROUP_SIZE = 128
        EPS = 1e-06

        def _dequant_fp4(packed_i32, scales_f16, group_size):
            out_f, in_p = packed_i32.shape
            w = packed_i32.astype(jnp.uint32)
            shifts = jnp.arange(8, dtype=jnp.uint32) * 4
            nib = w[:, :, None] >> shifts & jnp.uint32(15)
            vals = _FP4_LUT[nib.astype(jnp.int32)].reshape(out_f, in_p * 8)
            s = scales_f16.astype(jnp.float32).T
            s_full = jnp.repeat(s, group_size, axis=1)
            return vals * s_full
        I = gate_up_packed.shape[0] // 2
        w_gu = _dequant_fp4(gate_up_packed, gate_up_scales, GROUP_SIZE)
        w_down = _dequant_fp4(down_packed, down_scales, GROUP_SIZE)
        gate_up = jnp.einsum('bsh,oh->bso', x, w_gu)
        gate, up = (gate_up[..., :I], gate_up[..., I:])
        h = jax.nn.silu(gate) * up
        y = jnp.einsum('bsi,hi->bsh', h, w_down)
        rms = jnp.sqrt(jnp.mean(y * y, axis=-1, keepdims=True) + EPS)
        return y / rms
    x = x + _L0_xattn_ref(_layernorm(x, axis=-1), ctx_2048, ctx_2048)
    x = x + _L0_ffn_ref(_layernorm(x, axis=-1), L0_ffn_gate_up_packed, L0_ffn_gate_up_scales, L0_ffn_down_packed, L0_ffn_down_scales)
    return x

_drawn_inputs = setup_inputs


def setup_inputs(seed=0):
    import zlib

    import numpy as np

    out = dict(_drawn_inputs(seed))
    spreads = {}
    factors = {}
    for name, (base, spread) in spreads.items():
        noise = np.random.default_rng([zlib.crc32(name.encode()), seed]).standard_normal(out[name].shape)
        drawn = base * np.exp(spread * noise) if base else spread * noise
        out[name] = jnp.asarray(drawn.astype(out[name].dtype))
    for name, factor in factors.items():
        out[name] = (out[name] * factor).astype(out[name].dtype)
    return out
```

```python
import concourse.bass as bass
from concourse import mybir
from contextlib import ExitStack

F32 = mybir.dt.float32
F32R = mybir.dt.float32r
F16 = mybir.dt.float16
U32 = mybir.dt.uint32
ALU = mybir.AluOpType
ACT = mybir.ActivationFunctionType
AXIS_X = mybir.AxisListType.X

P = 128
ROWS_PER_BATCH = 256
J = ROWS_PER_BATCH // P
RT = 2 * J
LN_EPS = 1e-5
RMS_EPS = 1e-6



def xattn_ffn_kernel(nc, x, ctx_in, gu_packed, gu_scales, dn_packed, dn_scales, out):
    B, S, D = x.shape
    I = dn_scales.shape[0] * P
    G = D // P
    T = I // P
    WG = P // 8
    MACROS = B // 2
    MACRO_ROWS = RT * P
    x_rows = x.rearrange("b s d -> (b s) d")
    ctx_rows = ctx_in.rearrange("b s d -> (b s) d")
    out_rows = out.rearrange("b s d -> (b s) d")

    GROUP_SUMS = T * 2 * G
    HALF_SUMS = GROUP_SUMS // 2

    GU_CHUNKS = [(0, 4), (4, 8), (8, 11)]
    DN_CHUNKS = [(0, 4), (4, 8), (8, 11)]
    CHUNK_USES = [2 * t0 for t0, _ in GU_CHUNKS] + [2 * T + g0 for g0, _ in DN_CHUNKS]
    CHUNK_WORDS = 2 * 4 * D // 8

    es = ExitStack()
    with es:
        def sb(name, shape, dt):
            return es.enter_context(nc.sbuf_tensor(name, shape, dt))

        def sem(name):
            return es.enter_context(nc.semaphore(name))

        gateupT = sb("gateupT", [P, G, 2, I], F32R)
        down_hi = sb("down_hi", [P, T, D], F32R)
        down_lo = sb("down_lo", [P, T, D], F32R)
        gu_scale = sb("gu_scale", [P, G, 2, T], F32)
        dn_scale = sb("dn_scale", [P, G, T], F32)
        ident32 = sb("ident32", [P, P], F32)
        ident16 = sb("ident16", [P, P], F16)
        minus_half = sb("minus_half", [P, RT], F32)
        x_sb = [sb(f"x_sb{b}", [P, J, D], F32) for b in range(2)]
        ctx_sb = [sb(f"ctx_sb{b}", [P, J, D], F32) for b in range(2)]
        xn_hi = sb("xn_hi", [P, J, D], F32R)
        xn_lo = sb("xn_lo", [P, J, D], F32R)
        ctx_hi = sb("ctx_hi", [P, J, D], F32R)
        ctx_lo = sb("ctx_lo", [P, J, D], F32R)
        work = sb("work", [P, 2, D], F32)
        exp_hi = sb("exp_hi", [P, G, D], F32R)
        exp_lo = sb("exp_lo", [P, G, D], F32R)
        ctxT_hi = sb("ctxT_hi", [P, G, ROWS_PER_BATCH], F32R)
        ctxT_lo = sb("ctxT_lo", [P, G, ROWS_PER_BATCH], F32R)
        x2_new = sb("x2_new", [P, RT, D], F32)
        xT_hi = sb("xT_hi", [P, G, MACRO_ROWS], F32R)
        xT_lo = sb("xT_lo", [P, G, MACRO_ROWS], F32R)
        bn = sb("bn", [P, 2, J, 6], F32)
        mv1 = sb("mv1", [P, J, 2], F32)
        mv2 = sb("mv2", [P, RT, 2], F32)
        var1 = sb("var1", [P, J], F32)
        var2 = sb("var2", [P, RT], F32)
        rstd1 = sb("rstd1", [P, J], F32)
        rstd2 = sb("rstd2", [P, RT], F32)
        neg_max = sb("neg_max", [P, G], F32)
        exp_sum = sb("exp_sum", [P, G], F32)
        inv_sum = sb("inv_sum", [P, G], F32)
        sq_sum = sb("sq_sum", [P, RT], F32)
        mean_sq = sb("mean_sq", [P, RT], F32)
        inv_rms = sb("inv_rms", [P, RT], F32)

        with ExitStack() as scratch:
            def tmp(name, shape, dt):
                return scratch.enter_context(nc.sbuf_tensor(name, shape, dt))

            gu_words = tmp("gu_words", [P, 2 * T, D // 8], U32)
            dn_words = tmp("dn_words", [P, G, I // 8], U32)
            sign_bits = tmp("sign_bits", [P, CHUNK_WORDS], U32)
            value_bits = tmp("value_bits", [P, CHUNK_WORDS], U32)
            planes = tmp("planes", [P, 4, CHUNK_WORDS], U32)
            values = tmp("values", [P, CHUNK_WORDS * 8], F16)
            diag = tmp("diag", [P, G, 4, P], F16)
            gu_scale_rows = tmp("gu_scale_rows", [G * 2 * T, P], F16)
            dn_scale_rows = tmp("dn_scale_rows", [T, D], F16)

        part_a = sb("part_a", [P, 2, MACRO_ROWS], F32)
        part_b = sb("part_b", [P, 2, MACRO_ROWS], F32)
        gate_up = sb("gate_up", [P, 2, MACRO_ROWS], F32)
        tanh_g = sb("tanh_g", [P, MACRO_ROWS], F32)
        h = sb("h", [P, MACRO_ROWS], F32)
        HBUF = 2
        h_hi = sb("h_hi", [P, HBUF, MACRO_ROWS], F32R)
        h_lo = sb("h_lo", [P, HBUF, MACRO_ROWS], F32R)
        x2_cur = sb("x2_cur", [P, RT, D], F32)
        square = sb("square", [P, D], F16)

        psD = [es.enter_context(nc.psum_tensor(f"psD{i}", [P, D], F32)) for i in range(RT)]
        psG = [es.enter_context(nc.psum_tensor(f"psG{i}", [P, D], F32)) for i in range(2)]
        psA = [es.enter_context(nc.psum_tensor(f"psA{i}", [P, D], F32)) for i in range(2)]
        turn_banks = [psG[0], psG[1], psA[0], psA[1]]

        x_in = [sem(f"x_in{b}") for b in range(2)]
        ctx_loaded = [sem(f"ctx_loaded{b}") for b in range(2)]
        gu_words_in = sem("gu_words_in")
        dn_words_in = sem("dn_words_in")
        scales_in = sem("scales_in")
        x2_copied = sem("x2_copied")
        out_stored = sem("out_stored")
        ident_made = sem("ident_made")
        scales_turned = sem("scales_turned")
        scales_ready = sem("scales_ready")
        bits_masked = sem("bits_masked")
        decoded = sem("decoded")
        reordered = sem("reordered")
        weights_turned = sem("weights_turned")
        gu_copied = sem("gu_copied")
        down_hi_done = sem("down_hi_done")
        down_lo_done = sem("down_lo_done")
        diag_made = sem("diag_made")
        ln1_stats = sem("ln1_stats")
        ln1_aggr = sem("ln1_aggr")
        ln1_var = sem("ln1_var")
        rstd1_done = sem("rstd1_done")
        xn_done = sem("xn_done")
        xn_hi_done = sem("xn_hi_done")
        xn_lo_done = sem("xn_lo_done")
        ctx_hi_done = sem("ctx_hi_done")
        ctx_lo_done = sem("ctx_lo_done")
        scores_done = sem("scores_done")
        max_done = sem("max_done")
        exp_done = sem("exp_done")
        exp_hi_done = sem("exp_hi_done")
        exp_lo_done = sem("exp_lo_done")
        inv_sum_done = sem("inv_sum_done")
        ctx_turned = sem("ctx_turned")
        ctxT_hi_done = sem("ctxT_hi_done")
        ctxT_lo_done = sem("ctxT_lo_done")
        mix_done = sem("mix_done")
        x2_done = sem("x2_done")
        ln2_stats = sem("ln2_stats")
        ln2_aggr = sem("ln2_aggr")
        ln2_var = sem("ln2_var")
        rstd2_done = sem("rstd2_done")
        xn2_done = sem("xn2_done")
        xn2_turned = sem("xn2_turned")
        xT_hi_done = sem("xT_hi_done")
        xT_lo_done = sem("xT_lo_done")
        group_sums = sem("group_sums")
        even_scaled = sem("even_scaled")
        odd_scaled = sem("odd_scaled")
        gate_up_done = sem("gate_up_done")
        tanh_done = sem("tanh_done")
        silu_done = sem("silu_done")
        h_done = sem("h_done")
        h_hi_done = sem("h_hi_done")
        h_lo_done = sem("h_lo_done")
        down_done = sem("down_done")
        squares_done = sem("squares_done")
        mean_sq_done = sem("mean_sq_done")
        inv_rms_done = sem("inv_rms_done")
        final_done = sem("final_done")

        block = es.enter_context(nc.Block())

        def later(count):
            return not isinstance(count, int) or count > 0

        def is_first(m):
            return isinstance(m, int) and m == 0

        def gu_chunk(c):
            t0, t1 = GU_CHUNKS[c]
            words = gu_words[:, :, :].rearrange("p (k t) w -> p k (t w)", k=2)
            return words[:, :, t0 * 64:t1 * 64], 2, (t1 - t0) * 64

        def dn_chunk(c):
            g0, g1 = DN_CHUNKS[c]
            return dn_words[:, :, g0 * WG:g1 * WG], G, (g1 - g0) * WG

        def down_users(m, t):
            before = t - HBUF if t >= HBUF else max(u for u in range(T) if u % HBUF == t % HBUF) - T
            return m * (T * RT) + (before + 1) * RT

        @block.sync
        def _(sp):
            def load_x(a, b):
                sp.dma_start(x_sb[b][:, :, :],
                             x_rows[bass.ds(a * MACRO_ROWS + b * ROWS_PER_BATCH, ROWS_PER_BATCH), :]
                             .rearrange("(j p) d -> p j d", p=P)).then_inc(x_in[b], 16)

            def load_ctx(a, b):
                sp.dma_start(ctx_sb[b][:, :, :],
                             ctx_rows[bass.ds(a * MACRO_ROWS + b * ROWS_PER_BATCH, ROWS_PER_BATCH), :]
                             .rearrange("(j p) d -> p j d", p=P)).then_inc(ctx_loaded[b], 16)

            def store(m):
                sp.wait_ge(final_done, m * RT + RT)
                sp.dma_start(out_rows[bass.ds(m * MACRO_ROWS, MACRO_ROWS), :].rearrange("(r p) d -> p r d", p=P),
                             x2_cur[:, :, :]).then_inc(out_stored, 16)

            def copy_x2(m):
                if later(m * 16):
                    sp.wait_ge(out_stored, m * 16)
                sp.wait_ge(x2_done, m * RT + RT)
                sp.dma_start(x2_cur[:, :, :], x2_new[:, :, :]).then_inc(x2_copied, 16)

            def next_loads(a):
                for b in range(2):
                    sp.wait_ge(x2_done, a * RT + J * (b + 1))
                    load_x(a + 1, b)
                sp.wait_ge(xn2_turned, a * G + G)
                for b in range(2):
                    load_ctx(a + 1, b)

            load_x(0, 0)
            sp.dma_start(gu_words[:, :, :], gu_packed.rearrange("(c p) w -> p c w", p=P)).then_inc(gu_words_in, 16)
            load_ctx(0, 0)
            sp.dma_start(gu_scale_rows[:, :], gu_scales.rearrange("g (c p) -> (g c) p", p=P)).then_inc(scales_in, 16)
            sp.dma_start(dn_scale_rows[:, :], dn_scales).then_inc(scales_in, 16)
            load_x(0, 1)
            load_ctx(0, 1)
            sp.dma_start(dn_words[:, :, :], dn_packed.rearrange("(c p) w -> p c w", p=P)).then_inc(dn_words_in, 16)
            next_loads(0)
            sp.wait_ge(down_lo_done, T)
            copy_x2(0)
            next_loads(1)
            with sp.Fori(1, MACROS - 2) as m:
                store(m - 1)
                copy_x2(m)
                next_loads(m + 1)
            for m in (MACROS - 2, MACROS - 1):
                store(m - 1)
                copy_x2(m)
            for rt in range(RT):
                sp.wait_ge(final_done, (MACROS - 1) * RT + rt + 1)
                row = (MACROS - 1) * MACRO_ROWS + rt * P
                sp.dma_start(out_rows[row:row + P, :], x2_cur[:, rt, :]).then_inc(out_stored, 16)
            sp.wait_ge(out_stored, 16 * (MACROS - 1 + RT))

        @block.tensor
        def _(pe):
            def three_passes(bank, stationary, moving, first, last):
                (s_hi, s_lo), (m_hi, m_lo) = stationary, moving
                nc.tensor.matmul(bank, s_hi, m_hi, start=first, stop=False)
                nc.tensor.matmul(bank, s_lo, m_hi, start=False, stop=False)
                return nc.tensor.matmul(bank, s_hi, m_lo, start=False, stop=last)

            def scores(a, b, e):
                q = a * 2 + b
                pe.wait_ge(xn_lo_done, q * J + J)
                pe.wait_ge(ctx_lo_done, q * J + J)
                if e < 2:
                    if b == 0:
                        if later(a * G):
                            pe.wait_ge(xT_lo_done, a * G)
                    else:
                        pe.wait_ge(x2_done, q * J)
                else:
                    pe.wait_ge(exp_done, q * G + e - 1)
                for j in range(J):
                    last = three_passes(psA[e % 2][:, :],
                                        (ctx_hi[:, j, e * P:(e + 1) * P], ctx_lo[:, j, e * P:(e + 1) * P]),
                                        (xn_hi[:, j, :], xn_lo[:, j, :]), j == 0, j == J - 1)
                last.then_inc(scores_done, 1)

            def turn_ctx(a, b, pair):
                q = a * 2 + b
                pe.wait_ge(exp_done, q * G + 3 + pair)
                for k in range(2):
                    for j in range(J):
                        e = 2 * pair + k
                        last = nc.tensor.transpose(psA[pair][:, (k * J + j) * P:(k * J + j + 1) * P],
                                                   ctx_sb[b][:, j, e * P:(e + 1) * P], ident32[:, :])
                last.then_inc(ctx_turned, 1)

            def mix(a, b, j, e):
                q = a * 2 + b
                if e == 0:
                    pe.wait_ge(ctxT_lo_done, q * G + G)
                    pe.wait_ge(exp_lo_done, q * G + G)
                last = three_passes(psA[j][:, :],
                                    (ctxT_hi[:, e, j * P:(j + 1) * P], ctxT_lo[:, e, j * P:(j + 1) * P]),
                                    (exp_hi[:, e, :], exp_lo[:, e, :]), e == 0, e == G - 1)
                if e == G - 1:
                    last.then_inc(mix_done, 1)

            def turn_xn2(a):
                pe.wait_ge(xn2_done, a * RT + RT)
                if later(a * HALF_SUMS):
                    pe.wait_ge(even_scaled, a * HALF_SUMS)
                if later(a * HALF_SUMS):
                    pe.wait_ge(odd_scaled, a * HALF_SUMS)
                for k in range(G):
                    for rt in range(RT):
                        last = nc.tensor.transpose(turn_banks[k][:, rt * P:(rt + 1) * P],
                                                   ctx_sb[rt // J][:, rt % J, k * P:(k + 1) * P], ident32[:, :])
                    last.then_inc(xn2_turned, 1)

            def group_sum(m, t, n):
                k, g = n // G, n % G
                done = m * HALF_SUMS + (t * 8 + n) // 2
                if later(done):
                    pe.wait_ge(even_scaled if n % 2 == 0 else odd_scaled, done)
                if t == 0 and k == 0:
                    pe.wait_ge(xT_lo_done, m * G + g + 1)
                if is_first(m) and t == 0 and n == 0:
                    pe.wait_ge(gu_copied, 2 * T)
                w = gateupT[:, g, k, t * P:(t + 1) * P]
                nc.tensor.matmul(psG[n % 2][:, :], w, xT_hi[:, g, :], start=True, stop=False)
                nc.tensor.matmul(psG[n % 2][:, :], w, xT_lo[:, g, :], start=False, stop=True).then_inc(group_sums, 1)

            def down(m, t, rt):
                if rt == 0:
                    pe.wait_ge(h_lo_done, m * T + t + 1)
                if t == 0:
                    if later(m * RT - RT + rt + 1):
                        pe.wait_ge(final_done, m * RT - RT + rt + 1)
                if is_first(m) and t == 0 and rt == 0:
                    pe.wait_ge(down_lo_done, T)
                cols = slice(rt * P, (rt + 1) * P)
                three_passes(psD[rt][:, :], (h_hi[:, t % HBUF, cols], h_lo[:, t % HBUF, cols]),
                             (down_hi[:, t, :], down_lo[:, t, :]), t == 0, t == T - 1).then_inc(down_done, 1)

            def turn_weights(c):
                pe.wait_ge(reordered, c + 1)
                if c < len(GU_CHUNKS):
                    t0, t1 = GU_CHUNKS[c]
                    for i in range(2 * (t1 - t0)):
                        use = 2 * t0 + i
                        if later(use - RT + 1):
                            pe.wait_ge(gu_copied, use - RT + 1)
                        for g in range(G):
                            last = nc.tensor.matmul(psD[use % RT][:, g * P:(g + 1) * P],
                                                    values[:, i * D + g * P:i * D + (g + 1) * P], ident16[:, :],
                                                    start=True, stop=True)
                        last.then_inc(weights_turned, 1)
                else:
                    g0, g1 = DN_CHUNKS[c - len(GU_CHUNKS)]
                    pe.wait_ge(diag_made, c - len(GU_CHUNKS) + 1)
                    for g in range(g0, g1):
                        use = 2 * T + g
                        if use - RT < 2 * T:
                            pe.wait_ge(gu_copied, use - RT + 1)
                        else:
                            pe.wait_ge(down_lo_done, g - RT + 1)
                        for o in range(G):
                            at = (o * (g1 - g0) + g - g0) * P
                            last = nc.tensor.matmul(psD[use % RT][:, o * P:(o + 1) * P], values[:, at:at + P],
                                                    diag[:, o, g - g0, :], start=True, stop=True)
                        last.then_inc(weights_turned, 1)

            def attention(a, t, n):
                if (t, n) == (1, 5):
                    scores(a, 0, 0)
                elif (t, n) == (2, 1):
                    scores(a, 0, 1)
                elif (t, n) == (2, 5):
                    scores(a, 0, 2)
                elif (t, n) == (3, 1):
                    scores(a, 0, 3)
                elif (t, n) == (3, 6):
                    turn_ctx(a, 0, 0)
                elif (t, n) == (3, 7):
                    turn_ctx(a, 0, 1)
                elif (t, n) == (4, 5):
                    mix(a, 0, 0, 0)
                elif (t, n) == (4, 6):
                    mix(a, 0, 0, 1)
                elif (t, n) == (4, 7):
                    mix(a, 0, 0, 2)
                elif (t, n) == (5, 0):
                    mix(a, 0, 0, 3)
                elif (t, n) == (5, 2):
                    mix(a, 0, 1, 0)
                elif (t, n) == (5, 4):
                    mix(a, 0, 1, 1)
                elif (t, n) == (5, 6):
                    mix(a, 0, 1, 2)
                elif (t, n) == (5, 7):
                    mix(a, 0, 1, 3)
                elif (t, n) == (6, 1):
                    scores(a, 1, 0)
                elif (t, n) == (6, 5):
                    scores(a, 1, 1)
                elif (t, n) == (7, 1):
                    scores(a, 1, 2)
                elif (t, n) == (7, 5):
                    scores(a, 1, 3)
                elif (t, n) == (8, 1):
                    turn_ctx(a, 1, 0)
                elif (t, n) == (8, 2):
                    turn_ctx(a, 1, 1)
                elif (t, n) == (8, 6):
                    mix(a, 1, 0, 0)
                elif (t, n) == (8, 7):
                    mix(a, 1, 0, 1)
                elif (t, n) == (9, 0):
                    mix(a, 1, 0, 2)
                elif (t, n) == (9, 1):
                    mix(a, 1, 0, 3)
                elif (t, n) == (9, 3):
                    mix(a, 1, 1, 0)
                elif (t, n) == (9, 4):
                    mix(a, 1, 1, 1)
                elif (t, n) == (9, 5):
                    mix(a, 1, 1, 2)
                elif (t, n) == (9, 6):
                    mix(a, 1, 1, 3)

            def ffn(m, attend):
                for t in range(T):
                    for n in range(2 * G):
                        group_sum(m, t, n)
                        if t == 0 and n % 2 and not is_first(m):
                            down(m - 1, T - 2, n // 2)
                        if t == 1 and n < RT and not is_first(m):
                            down(m - 1, T - 1, n)
                        if t == 2 and n >= RT:
                            down(m, 0, n - RT)
                        if t > 2 and n % 2:
                            down(m, t - 2, n // 2)
                        if attend:
                            attention(m + 1, t, n)
                if attend:
                    turn_xn2(m + 1)

            pe.wait_ge(scales_in, 32)
            pe.wait_ge(ident_made, 4)
            nc.tensor.matmul(psD[0][:, 0:G * 2 * T], gu_scale_rows[:, :], ident16[0:G * 2 * T, 0:G * 2 * T],
                             start=True, stop=True).then_inc(scales_turned, 1)
            for o in range(G):
                last = nc.tensor.matmul(psD[1][:, o * T:(o + 1) * T], dn_scale_rows[:, o * P:(o + 1) * P],
                                        ident16[0:T, 0:T], start=True, stop=True)
            last.then_inc(scales_turned, 1)
            for e in range(G):
                scores(0, 0, e)
            pe.wait_ge(scales_ready, 2)
            turn_weights(0)
            for pair in range(2):
                turn_ctx(0, 0, pair)
            for j in range(J):
                for e in range(G):
                    mix(0, 0, j, e)
            turn_weights(1)
            for e in range(G):
                scores(0, 1, e)
            turn_weights(2)
            for pair in range(2):
                turn_ctx(0, 1, pair)
            for j in range(J):
                for e in range(G):
                    mix(0, 1, j, e)
            turn_weights(3)
            turn_xn2(0)
            turn_weights(4)
            turn_weights(5)
            ffn(0, True)
            with pe.Fori(1, MACROS - 1) as m:
                ffn(m, True)
            ffn(MACROS - 1, False)
            for t in (T - 2, T - 1):
                for rt in range(RT):
                    down(MACROS - 1, t, rt)

        @block.vector
        def _(dve):
            def layer_norm_stats(src, mean_var, var, half, names, q, scale):
                stats_sem, aggr_sem, var_sem = names
                for j in range(J):
                    nc.vector.bn_stats(bn[:, half, j, :], src(j)).then_inc(stats_sem, 1)
                dve.wait_ge(stats_sem, q * J + J)
                nc.vector.memset(var, 0.0)
                for j in range(J):
                    nc.vector.bn_aggr(mean_var[:, j, :], bn[:, half, j, :]).then_inc(aggr_sem, 1)
                dve.wait_ge(aggr_sem, q * J + J)
                nc.vector.tensor_scalar(var, mean_var[:, :, 1], LN_EPS, scale, ALU.add, ALU.mult).then_inc(var_sem, 1)

            def ln1(a, b):
                dve.wait_ge(x_in[b], a * 16 + 16)
                layer_norm_stats(lambda j: x_sb[b][:, j, :], mv1[:, :, :], var1[:, :], 0,
                                 (ln1_stats, ln1_aggr, ln1_var), a * 2 + b, float(D))

            def normalise1(a, b):
                q = a * 2 + b
                dve.wait_ge(rstd1_done, q + 1)
                if later(q * G):
                    dve.wait_ge(exp_lo_done, q * G)
                for j in range(J):
                    nc.vector.tensor_scalar(work[:, j, :], x_sb[b][:, j, :], mv1[:, j, 0:1], rstd1[:, j:j + 1],
                                            ALU.subtract, ALU.mult).then_inc(xn_done, 1)

            def maximum(a, b, e):
                q = a * 2 + b
                dve.wait_ge(scores_done, q * G + e + 1)
                nc.vector.tensor_reduce(neg_max[:, e:e + 1], psA[e % 2][:, :], AXIS_X, ALU.max,
                                        negate=True).then_inc(max_done, 1)

            def inverse_sums(a, b):
                q = a * 2 + b
                dve.wait_ge(exp_done, q * G + G)
                nc.vector.reciprocal(inv_sum[:, :], exp_sum[:, :]).then_inc(inv_sum_done, 1)

            def split_ctxT(a, b, pair):
                q = a * 2 + b
                dve.wait_ge(ctx_turned, q * 2 + pair + 1)
                if pair == 0:
                    dve.wait_ge(inv_sum_done, q + 1)
                    if later(q * J):
                        dve.wait_ge(mix_done, q * J)
                for k in range(2):
                    e = 2 * pair + k
                    nc.vector.tensor_scalar(ctxT_hi[:, e, :], psA[pair][:, k * 256:(k + 1) * 256],
                                            inv_sum[:, e:e + 1], None, ALU.mult).then_inc(ctxT_hi_done, 1)
                for k in range(2):
                    e = 2 * pair + k
                    dve.wait_ge(ctxT_hi_done, q * G + e + 1)
                    nc.vector.scalar_tensor_tensor(out=ctxT_lo[:, e, :], in0=psA[pair][:, k * 256:(k + 1) * 256],
                                                   scalar=inv_sum[:, e:e + 1], in1=ctxT_hi[:, e, :].bitcast(F32),
                                                   op0=ALU.mult, op1=ALU.subtract).then_inc(ctxT_lo_done, 1)

            def residual(a, b, j):
                q = a * 2 + b
                dve.wait_ge(mix_done, q * J + j + 1)
                if later(a * 16):
                    dve.wait_ge(x2_copied, a * 16)
                nc.vector.tensor_tensor(x2_new[:, J * b + j, :], psA[j][:, :], x_sb[b][:, j, :],
                                        ALU.add).then_inc(x2_done, 1)

            def ln2(a, b):
                q = a * 2 + b
                dve.wait_ge(x2_done, q * J + J)
                layer_norm_stats(lambda j: x2_new[:, J * b + j, :], mv2[:, J * b:J * b + J, :],
                                 var2[:, J * b:J * b + J], 1, (ln2_stats, ln2_aggr, ln2_var), q, 1.0)

            def normalise2(a, b):
                q = a * 2 + b
                dve.wait_ge(rstd2_done, q + 1)
                for j in range(J):
                    rt = J * b + j
                    nc.vector.tensor_scalar(ctx_sb[b][:, j, :], x2_new[:, rt, :], mv2[:, rt, 0:1],
                                            rstd2[:, rt:rt + 1], ALU.subtract, ALU.mult).then_inc(xn2_done, 1)

            def split_xT(a):
                for k in range(G):
                    dve.wait_ge(xT_hi_done, a * G + k + 1)
                    nc.vector.tensor_tensor(xT_lo[:, k, :], turn_banks[k][:, :], xT_hi[:, k, :].bitcast(F32),
                                            ALU.subtract).then_inc(xT_lo_done, 1)

            def scale_odd(m, t, n):
                k, g = n // G, n % G
                half = m * HALF_SUMS + (t * 8 + n) // 2
                dve.wait_ge(group_sums, m * GROUP_SUMS + t * 8 + n + 1)
                dve.wait_ge(even_scaled, half + 1)
                part = (part_a if g == 1 else part_b)[:, k, :]
                nc.vector.scalar_tensor_tensor(out=part, in0=psG[1][:, :], scalar=gu_scale[:, g, k, t:t + 1],
                                               in1=part, op0=ALU.mult, op1=ALU.add).then_inc(odd_scaled, 1)

            def silu(m, t):
                dve.wait_ge(tanh_done, m * T + t + 1)
                if later(m * T + t):
                    dve.wait_ge(h_lo_done, m * T + t)
                nc.vector.scalar_tensor_tensor(out=h[:, :], in0=tanh_g[:, :], scalar=1.0, in1=gate_up[:, 0, :],
                                               op0=ALU.add, op1=ALU.mult).then_inc(silu_done, 1)

            def times_up(m, t):
                dve.wait_ge(gate_up_done, m * (2 * T) + 2 * t + 2)
                dve.wait_ge(silu_done, m * T + t + 1)
                nc.vector.tensor_tensor(h[:, :], h[:, :], gate_up[:, 1, :], ALU.mult).then_inc(h_done, 1)

            def mean_squares(m):
                dve.wait_ge(squares_done, m * RT + RT)
                nc.vector.tensor_scalar(mean_sq[:, :], sq_sum[:, :], 1.0 / D, RMS_EPS, ALU.mult,
                                        ALU.add).then_inc(mean_sq_done, 1)

            def finish(m, rt):
                dve.wait_ge(inv_rms_done, m + 1)
                dve.wait_ge(x2_copied, m * 16 + 16)
                nc.vector.scalar_tensor_tensor(out=x2_cur[:, rt, :], in0=psD[rt][:, :], scalar=inv_rms[:, rt:rt + 1],
                                               in1=x2_cur[:, rt, :], op0=ALU.mult, op1=ALU.add).then_inc(final_done, 1)

            def decode(c):
                words, a, n = gu_chunk(c) if c < len(GU_CHUNKS) else dn_chunk(c - len(GU_CHUNKS))
                dve.wait_ge(gu_words_in if c < len(GU_CHUNKS) else dn_words_in, 16)
                if later(c):
                    dve.wait_ge(reordered, c)

                def view(t):
                    return t[:, 0:a * n].rearrange("p (a n) -> p a n", a=a)

                for i in range(4):
                    if later(4 * c + i):
                        dve.wait_ge(decoded, 4 * c + i)
                    nc.vector.tensor_scalar(view(sign_bits), words, 12 - 4 * i, 0x80008000,
                                            ALU.logical_shift_left, ALU.bitwise_and).then_inc(bits_masked, 1)
                    shift = ALU.logical_shift_left if i < 3 else ALU.logical_shift_right
                    nc.vector.tensor_scalar(view(value_bits), words, abs(9 - 4 * i), 0x0E000E00,
                                            shift, ALU.bitwise_and).then_inc(bits_masked, 1)
                    dve.wait_ge(bits_masked, 2 * (4 * c + i) + 2)
                    nc.vector.tensor_tensor(planes[:, i, 0:a * n], sign_bits[:, 0:a * n], value_bits[:, 0:a * n],
                                            ALU.bitwise_or).then_inc(decoded, 1)

            def down_rest(c):
                for g in range(*DN_CHUNKS[c]):
                    use = 2 * T + g
                    dve.wait_ge(down_hi_done, g + 1)
                    nc.vector.scalar_tensor_tensor(out=down_lo[:, g, :], in0=psD[use % RT][:, :], scalar=16384.0,
                                                   in1=down_hi[:, g, :].bitcast(F32), op0=ALU.mult,
                                                   op1=ALU.subtract).then_inc(down_lo_done, 1)

            def attention(a, t, n):
                if (t, n) == (0, 3):
                    ln1(a, 0)
                elif (t, n) == (0, 7):
                    normalise1(a, 0)
                elif (t, n) == (1, 7):
                    maximum(a, 0, 0)
                elif (t, n) == (2, 3):
                    maximum(a, 0, 1)
                elif (t, n) == (2, 7):
                    maximum(a, 0, 2)
                elif (t, n) == (3, 3):
                    maximum(a, 0, 3)
                elif (t, n) == (3, 7):
                    inverse_sums(a, 0)
                elif (t, n) == (4, 1):
                    split_ctxT(a, 0, 0)
                elif (t, n) == (4, 3):
                    split_ctxT(a, 0, 1)
                elif (t, n) == (4, 5):
                    ln1(a, 1)
                elif (t, n) == (4, 7):
                    normalise1(a, 1)
                elif (t, n) == (5, 3):
                    residual(a, 0, 0)
                elif (t, n) == (6, 1):
                    residual(a, 0, 1)
                elif (t, n) == (6, 3):
                    maximum(a, 1, 0)
                elif (t, n) == (6, 5):
                    ln2(a, 0)
                elif (t, n) == (6, 7):
                    maximum(a, 1, 1)
                elif (t, n) == (7, 3):
                    maximum(a, 1, 2)
                elif (t, n) == (7, 5):
                    normalise2(a, 0)
                elif (t, n) == (7, 7):
                    maximum(a, 1, 3)
                elif (t, n) == (8, 1):
                    inverse_sums(a, 1)
                elif (t, n) == (8, 3):
                    split_ctxT(a, 1, 0)
                elif (t, n) == (8, 5):
                    split_ctxT(a, 1, 1)
                elif (t, n) == (9, 3):
                    residual(a, 1, 0)
                elif (t, n) == (9, 7):
                    residual(a, 1, 1)
                elif (t, n) == (10, 1):
                    ln2(a, 1)
                elif (t, n) == (10, 5):
                    normalise2(a, 1)

            def ffn(m, attend):
                first = is_first(m)
                for t in range(T):
                    for n in range(1, 2 * G, 2):
                        scale_odd(m, t, n)
                        if n == 1 and t > 0:
                            times_up(m, t - 1)
                        if n == 1 and t == 0 and not first:
                            times_up(m - 1, T - 1)
                        if n == 7:
                            silu(m, t)
                        if not first:
                            if (t, n) == (1, 7):
                                mean_squares(m - 1)
                            if (t, n) == (2, 1):
                                finish(m - 1, 0)
                                finish(m - 1, 1)
                            if (t, n) == (2, 3):
                                finish(m - 1, 2)
                                finish(m - 1, 3)
                        if attend:
                            attention(m + 1, t, n)
                if attend:
                    split_xT(m + 1)

            ln1(0, 0)
            normalise1(0, 0)
            dve.wait_ge(scales_turned, 1)
            turned = psD[0][:, 0:G * 2 * T].rearrange("p (g k t) -> p g k t", g=G, k=2)
            for k in range(2):
                last = nc.vector.tensor_scalar(gu_scale[:, :, k, :], turned[:, :, k, :], 0.5 if k else 1.0, None, ALU.mult)
            last.then_inc(scales_ready, 1)
            dve.wait_ge(scales_turned, 2)
            nc.vector.tensor_copy(dn_scale[:, :, :].rearrange("p o g -> p (o g)"),
                                  psD[1][:, 0:G * T]).then_inc(scales_ready, 1)
            decode(0)
            for e in range(G):
                maximum(0, 0, e)
            decode(1)
            inverse_sums(0, 0)
            for pair in range(2):
                split_ctxT(0, 0, pair)
            for j in range(J):
                residual(0, 0, j)
            ln2(0, 0)
            ln1(0, 1)
            normalise2(0, 0)
            normalise1(0, 1)
            decode(2)
            for e in range(G):
                maximum(0, 1, e)
            decode(3)
            inverse_sums(0, 1)
            for pair in range(2):
                split_ctxT(0, 1, pair)
            for j in range(J):
                residual(0, 1, j)
            ln2(0, 1)
            normalise2(0, 1)
            down_rest(0)
            split_xT(0)
            decode(4)
            down_rest(1)
            decode(5)
            down_rest(2)
            ffn(0, True)
            with dve.Fori(1, MACROS - 1) as m:
                ffn(m, True)
            ffn(MACROS - 1, False)
            times_up(MACROS - 1, T - 1)
            mean_squares(MACROS - 1)
            for rt in range(RT):
                finish(MACROS - 1, rt)

        @block.scalar
        def _(act):
            def xn_high(a, b):
                q = a * 2 + b
                if later(q * G):
                    act.wait_ge(scores_done, q * G)
                for j in range(J):
                    act.wait_ge(xn_done, q * J + j + 1)
                    nc.scalar.activation(xn_hi[:, j, :], work[:, j, :], ACT.Copy).then_inc(xn_hi_done, 1)

            def ctx_high(a, b):
                q = a * 2 + b
                act.wait_ge(ctx_loaded[b], a * 16 + 16)
                if later(q * G):
                    act.wait_ge(scores_done, q * G)
                for j in range(J):
                    nc.scalar.activation(ctx_hi[:, j, :], ctx_sb[b][:, j, :], ACT.Copy).then_inc(ctx_hi_done, 1)

            def exponent(a, b, e):
                q = a * 2 + b
                act.wait_ge(max_done, q * G + e + 1)
                if later(q):
                    act.wait_ge(inv_sum_done, q)
                if e < 2:
                    act.wait_ge(xn_lo_done, q * J + J)
                else:
                    act.wait_ge(exp_lo_done, q * G + e - 1)
                nc.scalar.activation(work[:, e % 2, :], psA[e % 2][:, :], ACT.Exp, bias=neg_max[:, e:e + 1],
                                     accum_out=exp_sum[:, e:e + 1]).then_inc(exp_done, 1)
                act.wait_ge(exp_done, q * G + e + 1)
                if later(q * J):
                    act.wait_ge(mix_done, q * J)
                nc.scalar.activation(exp_hi[:, e, :], work[:, e % 2, :], ACT.Copy).then_inc(exp_hi_done, 1)

            def xT_high(a):
                for k in range(G):
                    act.wait_ge(xn2_turned, a * G + k + 1)
                    nc.scalar.activation(xT_hi[:, k, :], turn_banks[k][:, :], ACT.Copy).then_inc(xT_hi_done, 1)

            def scale_even(m, t, n):
                k, g = n // G, n % G
                act.wait_ge(group_sums, m * GROUP_SUMS + t * 8 + n + 1)
                if later(m * (2 * T) + 2 * t + k - 1):
                    act.wait_ge(gate_up_done, m * (2 * T) + 2 * t + k - 1)
                part = (part_a if g == 0 else part_b)[:, k, :]
                nc.scalar.activation(part, psG[0][:, :], ACT.Copy, scale=gu_scale[:, g, k, t:t + 1]).then_inc(even_scaled, 1)

            def tanh(m, t):
                act.wait_ge(gate_up_done, m * (2 * T) + 2 * t + 1)
                if later(m * T + t):
                    act.wait_ge(silu_done, m * T + t)
                nc.scalar.activation(tanh_g[:, :], gate_up[:, 0, :], ACT.Tanh, scale=0.5).then_inc(tanh_done, 1)

            def h_high(m, t):
                act.wait_ge(h_done, m * T + t + 1)
                if later(down_users(m, t)):
                    act.wait_ge(down_done, down_users(m, t))
                nc.scalar.activation(h_hi[:, t % HBUF, :], h[:, :], ACT.Copy).then_inc(h_hi_done, 1)

            def squares(m, rt):
                act.wait_ge(down_done, m * (T * RT) + (T - 1) * RT + rt + 1)
                act.wait_ge(mean_sq_done, m)
                act.wait_ge(squares_done, m * RT + rt)
                nc.scalar.activation(square[:, :], psD[rt][:, :], ACT.Square,
                                     accum_out=sq_sum[:, rt:rt + 1]).then_inc(squares_done, 1)

            def reorder(c):
                n = (gu_chunk(c) if c < len(GU_CHUNKS) else dn_chunk(c - len(GU_CHUNKS)))
                n = n[1] * n[2]
                act.wait_ge(decoded, 4 * c + 4)
                if later(CHUNK_USES[c]):
                    act.wait_ge(weights_turned, CHUNK_USES[c])
                nc.scalar.activation(values[:, 0:8 * n].rearrange("p (q i) -> p i q", i=4),
                                     planes[:, :, 0:n].bitcast(F16), ACT.Copy).then_inc(reordered, 1)

            def copy_weights(c):
                if c < len(GU_CHUNKS):
                    t0, t1 = GU_CHUNKS[c]
                    for k in range(2):
                        for t in range(t0, t1):
                            use = 2 * t0 + k * (t1 - t0) + t - t0
                            act.wait_ge(weights_turned, use + 1)
                            nc.scalar.activation(gateupT[:, :, k, t * P:(t + 1) * P],
                                                 psD[use % RT][:, :].rearrange("p (g o) -> p g o", g=G),
                                                 ACT.Copy, scale=16384.0).then_inc(gu_copied, 1)
                else:
                    for g in range(*DN_CHUNKS[c - len(GU_CHUNKS)]):
                        use = 2 * T + g
                        act.wait_ge(weights_turned, use + 1)
                        nc.scalar.activation(down_hi[:, g, :], psD[use % RT][:, :], ACT.Copy,
                                             scale=16384.0).then_inc(down_hi_done, 1)

            def attention(a, t, n):
                if (t, n) == (0, 6):
                    ctx_high(a, 0)
                elif (t, n) == (1, 0):
                    xn_high(a, 0)
                elif (t, n) == (2, 0):
                    exponent(a, 0, 0)
                elif (t, n) == (2, 4):
                    exponent(a, 0, 1)
                elif (t, n) == (3, 0):
                    exponent(a, 0, 2)
                elif (t, n) == (3, 4):
                    exponent(a, 0, 3)
                elif (t, n) == (4, 6):
                    ctx_high(a, 1)
                elif (t, n) == (5, 0):
                    xn_high(a, 1)
                elif (t, n) == (6, 4):
                    exponent(a, 1, 0)
                elif (t, n) == (7, 0):
                    exponent(a, 1, 1)
                elif (t, n) == (7, 4):
                    exponent(a, 1, 2)
                elif (t, n) == (8, 0):
                    exponent(a, 1, 3)

            def ffn(m, attend):
                first = is_first(m)
                for t in range(T):
                    for n in range(0, 2 * G, 2):
                        scale_even(m, t, n)
                        if n == 2 and t > 0:
                            h_high(m, t - 1)
                        if n == 2 and t == 0 and not first:
                            h_high(m - 1, T - 1)
                        if n == 4:
                            tanh(m, t)
                        if t == 1 and n >= 4 and not first:
                            squares(m - 1, n - 4)
                            squares(m - 1, n - 3)
                        if attend:
                            attention(m + 1, t, n)
                if attend:
                    xT_high(m + 1)

            ctx_high(0, 0)
            xn_high(0, 0)
            reorder(0)
            for e in range(G):
                exponent(0, 0, e)
            copy_weights(0)
            reorder(1)
            ctx_high(0, 1)
            xn_high(0, 1)
            copy_weights(1)
            reorder(2)
            for e in range(G):
                exponent(0, 1, e)
            copy_weights(2)
            reorder(3)
            copy_weights(3)
            xT_high(0)
            reorder(4)
            copy_weights(4)
            reorder(5)
            copy_weights(5)
            ffn(0, True)
            with act.Fori(1, MACROS - 1) as m:
                ffn(m, True)
            ffn(MACROS - 1, False)
            h_high(MACROS - 1, T - 1)
            for rt in range(RT):
                squares(MACROS - 1, rt)

        @block.gpsimd
        def _(pool):
            def rstd_1(a, b):
                q = a * 2 + b
                pool.wait_ge(ln1_var, q + 1)
                nc.gpsimd.tensor_tensor(rstd1[:, :], var1[:, :], minus_half[:, 0:J], ALU.pow).then_inc(rstd1_done, 1)

            def rstd_2(a, b):
                q = a * 2 + b
                pool.wait_ge(ln2_var, q + 1)
                nc.gpsimd.tensor_tensor(rstd2[:, J * b:J * b + J], var2[:, J * b:J * b + J], minus_half[:, 0:J],
                                        ALU.pow).then_inc(rstd2_done, 1)

            def xn_low(a, b):
                q = a * 2 + b
                for j in range(J):
                    pool.wait_ge(xn_hi_done, q * J + j + 1)
                    nc.gpsimd.tensor_tensor(xn_lo[:, j, :], work[:, j, :], xn_hi[:, j, :].bitcast(F32),
                                            ALU.subtract).then_inc(xn_lo_done, 1)

            def ctx_low(a, b):
                q = a * 2 + b
                for j in range(J):
                    pool.wait_ge(ctx_hi_done, q * J + j + 1)
                    nc.gpsimd.tensor_tensor(ctx_lo[:, j, :], ctx_sb[b][:, j, :], ctx_hi[:, j, :].bitcast(F32),
                                            ALU.subtract).then_inc(ctx_lo_done, 1)

            def exp_low(a, b, e):
                q = a * 2 + b
                pool.wait_ge(exp_hi_done, q * G + e + 1)
                nc.gpsimd.tensor_tensor(exp_lo[:, e, :], work[:, e % 2, :], exp_hi[:, e, :].bitcast(F32),
                                        ALU.subtract).then_inc(exp_lo_done, 1)

            def add_parts(m, t, k):
                pool.wait_ge(odd_scaled, m * HALF_SUMS + t * G + 2 * k + 2)
                if k == 0:
                    if later(m * T + t):
                        pool.wait_ge(silu_done, m * T + t)
                else:
                    if later(m * T + t):
                        pool.wait_ge(h_done, m * T + t)
                nc.gpsimd.tensor_tensor(gate_up[:, k, :], part_a[:, k, :], part_b[:, k, :],
                                        ALU.add).then_inc(gate_up_done, 1)

            def h_low(m, t):
                pool.wait_ge(h_hi_done, m * T + t + 1)
                nc.gpsimd.tensor_tensor(h_lo[:, t % HBUF, :], h[:, :], h_hi[:, t % HBUF, :].bitcast(F32),
                                        ALU.subtract).then_inc(h_lo_done, 1)

            def inverse_rms(m):
                pool.wait_ge(mean_sq_done, m + 1)
                nc.gpsimd.tensor_tensor(inv_rms[:, :], mean_sq[:, :], minus_half[:, :], ALU.pow).then_inc(inv_rms_done, 1)

            def diagonals(c):
                g0, g1 = DN_CHUNKS[c]
                pool.wait_ge(scales_ready, 2)
                if later(CHUNK_USES[len(GU_CHUNKS) + c] if c else 0):
                    pool.wait_ge(weights_turned, CHUNK_USES[len(GU_CHUNKS) + c] if c else 0)
                for o in range(G):
                    last = nc.gpsimd.tensor_tensor(
                        diag[:, o, 0:g1 - g0, :], ident16[:, :].unsqueeze(1).broadcast_to([P, g1 - g0, P]),
                        dn_scale[:, o, g0:g1].unsqueeze(2).broadcast_to([P, g1 - g0, P]), ALU.mult)
                last.then_inc(diag_made, 1)

            def attention(a, t, n):
                if (t, n) == (0, 5):
                    rstd_1(a, 0)
                elif (t, n) == (0, 7):
                    ctx_low(a, 0)
                elif (t, n) == (1, 1):
                    xn_low(a, 0)
                elif (t, n) == (2, 1):
                    exp_low(a, 0, 0)
                elif (t, n) == (2, 5):
                    exp_low(a, 0, 1)
                elif (t, n) == (3, 1):
                    exp_low(a, 0, 2)
                elif (t, n) == (3, 5):
                    exp_low(a, 0, 3)
                elif (t, n) == (4, 6):
                    rstd_1(a, 1)
                elif (t, n) == (5, 0):
                    ctx_low(a, 1)
                elif (t, n) == (5, 2):
                    xn_low(a, 1)
                elif (t, n) == (6, 5):
                    exp_low(a, 1, 0)
                    rstd_2(a, 0)
                elif (t, n) == (7, 1):
                    exp_low(a, 1, 1)
                elif (t, n) == (7, 5):
                    exp_low(a, 1, 2)
                elif (t, n) == (8, 1):
                    exp_low(a, 1, 3)
                elif (t, n) == (10, 2):
                    rstd_2(a, 1)

            def ffn(m, attend):
                first = is_first(m)
                for t in range(T):
                    for n in range(2 * G):
                        if n == 3:
                            add_parts(m, t, 0)
                        if n == 4 and t > 0:
                            h_low(m, t - 1)
                        if n == 4 and t == 0 and not first:
                            h_low(m - 1, T - 1)
                        if n == 7:
                            add_parts(m, t, 1)
                        if (t, n) == (1, 7) and not first:
                            inverse_rms(m - 1)
                        if attend:
                            attention(m + 1, t, n)

            for ident in (ident32, ident16):
                made = 0 if ident is ident32 else 2
                nc.gpsimd.memset(ident[:, :], 0.0).then_inc(ident_made, 1)
                pool.wait_ge(ident_made, made + 1)
                nc.gpsimd.affine_select(out=ident[:, :], in_=ident[:, :], compare_op=ALU.not_equal, fill=1.0, base=0,
                                        pattern=[[-1, P]], channel_multiplier=1).then_inc(ident_made, 1)
            nc.gpsimd.memset(minus_half[:, :], -0.5).then_inc(ident_made, 1)
            pool.wait_ge(ident_made, 5)
            rstd_1(0, 0)
            ctx_low(0, 0)
            xn_low(0, 0)
            for e in range(G):
                exp_low(0, 0, e)
            rstd_2(0, 0)
            rstd_1(0, 1)
            ctx_low(0, 1)
            xn_low(0, 1)
            for e in range(G):
                exp_low(0, 1, e)
            diagonals(0)
            rstd_2(0, 1)
            diagonals(1)
            diagonals(2)
            ffn(0, True)
            with pool.Fori(1, MACROS - 1) as m:
                ffn(m, True)
            ffn(MACROS - 1, False)
            h_low(MACROS - 1, T - 1)
            inverse_rms(MACROS - 1)


_INS = ['x', 'ctx_2048', 'L0_ffn_gate_up_packed', 'L0_ffn_gate_up_scales', 'L0_ffn_down_packed', 'L0_ffn_down_scales']
_OUTS = [((16, 256, 512), 'float32')]


def kernel(**inputs):
    import numpy as _np
    import concourse.bacc as _bacc
    from concourse import mybir as _mybir
    from concourse.bass_utils import run_bass_kernel_spmd as _run

    nc = _bacc.Bacc("TRN2", target_bir_lowering=False, num_devices=1)
    arrays, args = {}, []
    for name in _INS:
        a = _np.ascontiguousarray(inputs[name])
        if a.dtype == _np.int32:
            a = a.view(_np.uint32)
        arrays[f"in_{name}_dram"] = a
        args.append(nc.dram_tensor(f"in_{name}_dram", a.shape, _mybir.dt.from_np(a.dtype), kind="ExternalInput").ap())
    for i, (shape, dtype) in enumerate(_OUTS):
        dt = _mybir.dt.from_np(_np.dtype(dtype))
        args.append(nc.dram_tensor(f"out_{i}_dram", shape, dt, kind="ExternalOutput").ap())
    xattn_ffn_kernel(nc, *args)
    r = _run(nc, [arrays], core_ids=[0])
    got = tuple(r.results[0][f"out_{i}_dram"] for i in range(len(_OUTS)))
    return got[0]
```

```python
import concourse.bass as bass
from concourse import mybir
from contextlib import ExitStack

F32 = mybir.dt.float32
F32R = mybir.dt.float32r
F16 = mybir.dt.float16
U32 = mybir.dt.uint32
ALU = mybir.AluOpType
ACT = mybir.ActivationFunctionType
AXIS_X = mybir.AxisListType.X

P = 128
ROWS_PER_BATCH = 256
J = ROWS_PER_BATCH // P
RT = 2 * J
LN_EPS = 1e-5
RMS_EPS = 1e-6


def xattn_ffn_kernel(nc, x, ctx_in, gu_packed, gu_scales, dn_packed, dn_scales, out):
    B, S, D = x.shape
    I = dn_scales.shape[0] * P
    G = D // P
    T = I // P
    WG = P // 8
    MACROS = B // 2
    MACRO_ROWS = RT * P
    x_rows = x.rearrange("b s d -> (b s) d")
    ctx_rows = ctx_in.rearrange("b s d -> (b s) d")
    out_rows = out.rearrange("b s d -> (b s) d")

    GROUP_SUMS = T * 2 * G
    HALF_SUMS = GROUP_SUMS // 2

    GU_CHUNKS = [(0, 4), (4, 8), (8, 11)]
    DN_CHUNKS = [(0, 4), (4, 8), (8, 11)]
    CHUNK_USES = [2 * t0 for t0, _ in GU_CHUNKS] + [2 * T + g0 for g0, _ in DN_CHUNKS]
    CHUNK_WORDS = 2 * 4 * D // 8

    es = ExitStack()
    with es:
        def sb(name, shape, dt):
            return es.enter_context(nc.sbuf_tensor(name, shape, dt))

        def sem(name):
            return es.enter_context(nc.semaphore(name))

        gateupT = sb("gateupT", [P, G, 2, I], F32R)
        down_hi = sb("down_hi", [P, T, D], F32R)
        down_lo = sb("down_lo", [P, T, D], F32R)
        gu_scale = sb("gu_scale", [P, G, 2, T], F32)
        dn_scale = sb("dn_scale", [P, G, T], F32)
        ident32 = sb("ident32", [P, P], F32)
        ident16 = sb("ident16", [P, P], F16)
        minus_half = sb("minus_half", [P, RT], F32)
        x_sb = [sb(f"x_sb{b}", [P, J, D], F32) for b in range(2)]
        ctx_sb = [sb(f"ctx_sb{b}", [P, J, D], F32) for b in range(2)]
        xn_hi = sb("xn_hi", [P, J, D], F32R)
        xn_lo = sb("xn_lo", [P, J, D], F32R)
        ctx_hi = sb("ctx_hi", [P, J, D], F32R)
        ctx_lo = sb("ctx_lo", [P, J, D], F32R)
        work = sb("work", [P, 2, D], F32)
        exp_hi = sb("exp_hi", [P, G, D], F32R)
        exp_lo = sb("exp_lo", [P, G, D], F32R)
        ctxT_hi = sb("ctxT_hi", [P, G, ROWS_PER_BATCH], F32R)
        ctxT_lo = sb("ctxT_lo", [P, G, ROWS_PER_BATCH], F32R)
        x2_new = sb("x2_new", [P, RT, D], F32)
        xT_hi = sb("xT_hi", [P, G, MACRO_ROWS], F32R)
        xT_lo = sb("xT_lo", [P, G, MACRO_ROWS], F32R)
        bn = sb("bn", [P, 2, RT, 6], F32)
        mv1 = sb("mv1", [P, RT, 2], F32)
        mv2 = sb("mv2", [P, RT, 2], F32)
        var1 = sb("var1", [P, RT], F32)
        var2 = sb("var2", [P, RT], F32)
        rstd1 = sb("rstd1", [P, RT], F32)
        rstd2 = sb("rstd2", [P, RT], F32)
        neg_max = sb("neg_max", [P, G], F32)
        exp_sum = sb("exp_sum", [P, G], F32)
        inv_sum = sb("inv_sum", [P, G], F32)
        sq_sum = sb("sq_sum", [P, RT], F32)
        mean_sq = sb("mean_sq", [P, RT], F32)
        inv_rms = sb("inv_rms", [P, RT], F32)

        with ExitStack() as scratch:
            def tmp(name, shape, dt):
                return scratch.enter_context(nc.sbuf_tensor(name, shape, dt))

            gu_words = tmp("gu_words", [P, 2 * T, D // 8], U32)
            dn_words = tmp("dn_words", [P, G, I // 8], U32)
            sign_bits = tmp("sign_bits", [P, CHUNK_WORDS], U32)
            value_bits = tmp("value_bits", [P, CHUNK_WORDS], U32)
            planes = tmp("planes", [P, 4, CHUNK_WORDS], U32)
            values = tmp("values", [P, CHUNK_WORDS * 8], F16)
            with ExitStack() as rows_scratch:
                gu_scale_rows = rows_scratch.enter_context(nc.sbuf_tensor("gu_scale_rows", [G * 2 * T, P], F16))
                dn_scale_rows = rows_scratch.enter_context(nc.sbuf_tensor("dn_scale_rows", [T, D], F16))
            diag = tmp("diag", [P, G, 4, P], F16)

        part_a = sb("part_a", [P, 2, MACRO_ROWS], F32)
        part_b = sb("part_b", [P, 2, MACRO_ROWS], F32)
        gate_up = sb("gate_up", [P, 2, MACRO_ROWS], F32)
        tanh_g = sb("tanh_g", [P, MACRO_ROWS], F32)
        h = sb("h", [P, MACRO_ROWS], F32)
        HBUF = 2
        h_hi = sb("h_hi", [P, HBUF, MACRO_ROWS], F32R)
        h_lo = sb("h_lo", [P, HBUF, MACRO_ROWS], F32R)
        x2_cur = sb("x2_cur", [P, RT, D], F32)
        square = sb("square", [P, D], F16)

        def is_first(m):
            return isinstance(m, int) and m == 0

        psD = [es.enter_context(nc.psum_tensor(f"psD{i}", [P, D], F32)) for i in range(RT)]
        psG = [es.enter_context(nc.psum_tensor(f"psG{i}", [P, D], F32)) for i in range(2)]
        psA = [es.enter_context(nc.psum_tensor(f"psA{i}", [P, D], F32)) for i in range(2)]
        turn_banks = [psG[0], psG[1], psA[0], psA[1]]

        def banks(a, b):
            return psG if is_first(a) and b == 1 else psA


        x_in = [sem(f"x_in{b}") for b in range(2)]
        ctx_loaded = [sem(f"ctx_loaded{b}") for b in range(2)]
        gu_words_in = sem("gu_words_in")
        dn_words_in = sem("dn_words_in")
        scales_in = sem("scales_in")
        x2_copied = sem("x2_copied")
        out_stored = sem("out_stored")
        ident_made = sem("ident_made")
        scales_turned = sem("scales_turned")
        scales_ready = sem("scales_ready")
        bits_masked = sem("bits_masked")
        decoded = sem("decoded")
        reordered = sem("reordered")
        weights_turned = sem("weights_turned")
        gu_copied = sem("gu_copied")
        down_hi_done = sem("down_hi_done")
        down_lo_done = sem("down_lo_done")
        diag_made = sem("diag_made")
        ln1_stats = sem("ln1_stats")
        ln1_aggr = sem("ln1_aggr")
        ln1_var = sem("ln1_var")
        rstd1_done = sem("rstd1_done")
        xn_done = sem("xn_done")
        xn_hi_done = sem("xn_hi_done")
        xn_lo_done = sem("xn_lo_done")
        ctx_hi_done = sem("ctx_hi_done")
        ctx_lo_done = sem("ctx_lo_done")
        scores_done = sem("scores_done")
        max_done = sem("max_done")
        exp_done = sem("exp_done")
        exp_hi_done = sem("exp_hi_done")
        exp_lo_done = sem("exp_lo_done")
        inv_sum_done = sem("inv_sum_done")
        ctx_turned = sem("ctx_turned")
        ctxT_hi_done = sem("ctxT_hi_done")
        ctxT_lo_done = sem("ctxT_lo_done")
        mix_done = sem("mix_done")
        x2_done = sem("x2_done")
        ln2_stats = sem("ln2_stats")
        ln2_aggr = sem("ln2_aggr")
        ln2_var = sem("ln2_var")
        rstd2_done = sem("rstd2_done")
        xn2_done = sem("xn2_done")
        xn2_turned = sem("xn2_turned")
        xT_hi_done = sem("xT_hi_done")
        xT_lo_done = sem("xT_lo_done")
        group_sums = sem("group_sums")
        even_scaled = sem("even_scaled")
        odd_scaled = sem("odd_scaled")
        gate_up_done = sem("gate_up_done")
        tanh_done = sem("tanh_done")
        silu_done = sem("silu_done")
        h_done = sem("h_done")
        h_hi_done = sem("h_hi_done")
        h_lo_done = sem("h_lo_done")
        down_done = sem("down_done")
        squares_done = sem("squares_done")
        mean_sq_done = sem("mean_sq_done")
        inv_rms_done = sem("inv_rms_done")
        final_done = sem("final_done")

        block = es.enter_context(nc.Block())

        def later(count):
            return not isinstance(count, int) or count > 0

        def gu_chunk(c):
            t0, t1 = GU_CHUNKS[c]
            words = gu_words[:, :, :].rearrange("p (k t) w -> p k (t w)", k=2)
            return words[:, :, t0 * 64:t1 * 64], 2, (t1 - t0) * 64

        def dn_chunk(c):
            g0, g1 = DN_CHUNKS[c]
            return dn_words[:, :, g0 * WG:g1 * WG], G, (g1 - g0) * WG

        def down_users(m, t):
            before = t - HBUF if t >= HBUF else max(u for u in range(T) if u % HBUF == t % HBUF) - T
            return m * (T * RT) + (before + 1) * RT

        @block.sync
        def _(sp):
            def load_x(a, b):
                sp.dma_start(x_sb[b][:, :, :],
                             x_rows[bass.ds(a * MACRO_ROWS + b * ROWS_PER_BATCH, ROWS_PER_BATCH), :]
                             .rearrange("(j p) d -> p j d", p=P)).then_inc(x_in[b], 16)

            def load_ctx(a, b):
                sp.dma_start(ctx_sb[b][:, :, :],
                             ctx_rows[bass.ds(a * MACRO_ROWS + b * ROWS_PER_BATCH, ROWS_PER_BATCH), :]
                             .rearrange("(j p) d -> p j d", p=P)).then_inc(ctx_loaded[b], 16)

            def store(m):
                sp.wait_ge(final_done, m * RT + RT)
                sp.dma_start(out_rows[bass.ds(m * MACRO_ROWS, MACRO_ROWS), :].rearrange("(r p) d -> p r d", p=P),
                             x2_cur[:, :, :]).then_inc(out_stored, 16)

            def copy_x2(m):
                if later(m * 16):
                    sp.wait_ge(out_stored, m * 16)
                sp.wait_ge(x2_done, m * RT + RT)
                sp.dma_start(x2_cur[:, :, :], x2_new[:, :, :]).then_inc(x2_copied, 16)

            def next_loads(a):
                for b in range(2):
                    sp.wait_ge(x2_done, a * RT + J * (b + 1))
                    load_x(a + 1, b)
                sp.wait_ge(xn2_turned, a * G + G)
                for b in range(2):
                    load_ctx(a + 1, b)

            load_x(0, 0)
            sp.dma_start(gu_words[:, :, :], gu_packed.rearrange("(c p) w -> p c w", p=P)).then_inc(gu_words_in, 16)
            load_ctx(0, 0)
            sp.dma_start(gu_scale_rows[:, :], gu_scales.rearrange("g (c p) -> (g c) p", p=P)).then_inc(scales_in, 16)
            sp.dma_start(dn_scale_rows[:, :], dn_scales).then_inc(scales_in, 16)
            load_x(0, 1)
            load_ctx(0, 1)
            sp.dma_start(dn_words[:, :, :], dn_packed.rearrange("(c p) w -> p c w", p=P)).then_inc(dn_words_in, 16)
            next_loads(0)
            sp.wait_ge(down_lo_done, T)
            copy_x2(0)
            next_loads(1)
            with sp.Fori(1, MACROS - 2) as m:
                store(m - 1)
                copy_x2(m)
                next_loads(m + 1)
            for m in (MACROS - 2, MACROS - 1):
                store(m - 1)
                copy_x2(m)
            for rt in range(RT):
                sp.wait_ge(final_done, (MACROS - 1) * RT + rt + 1)
                row = (MACROS - 1) * MACRO_ROWS + rt * P
                sp.dma_start(out_rows[row:row + P, :], x2_cur[:, rt, :]).then_inc(out_stored, 16)
            sp.wait_ge(out_stored, 16 * (MACROS - 1 + RT))

        @block.tensor
        def _(pe):
            def three_passes(bank, stationary, moving, first, last):
                (s_hi, s_lo), (m_hi, m_lo) = stationary, moving
                nc.tensor.matmul(bank, s_hi, m_hi, start=first, stop=False)
                nc.tensor.matmul(bank, s_lo, m_hi, start=False, stop=False)
                return nc.tensor.matmul(bank, s_hi, m_lo, start=False, stop=last)

            def scores(a, b, e):
                q = a * 2 + b
                pe.wait_ge(xn_lo_done, q * J + J)
                pe.wait_ge(ctx_lo_done, q * J + J)
                if e < 2:
                    if b == 0:
                        if later(a * G):
                            pe.wait_ge(xT_lo_done, a * G)
                    elif not is_first(a):
                        pe.wait_ge(x2_done, q * J)
                else:
                    pe.wait_ge(exp_done, q * G + e - 1)
                for j in range(J):
                    last = three_passes(banks(a, b)[e % 2][:, :],
                                        (ctx_hi[:, j, e * P:(e + 1) * P], ctx_lo[:, j, e * P:(e + 1) * P]),
                                        (xn_hi[:, j, :], xn_lo[:, j, :]), j == 0, j == J - 1)
                last.then_inc(scores_done, 1)

            def turn_ctx(a, b, pair):
                q = a * 2 + b
                pe.wait_ge(exp_done, q * G + 3 + pair)
                for k in range(2):
                    for j in range(J):
                        e = 2 * pair + k
                        last = nc.tensor.transpose(banks(a, b)[pair][:, (k * J + j) * P:(k * J + j + 1) * P],
                                                   ctx_sb[b][:, j, e * P:(e + 1) * P], ident32[:, :])
                last.then_inc(ctx_turned, 1)

            def mix(a, b, j, e):
                q = a * 2 + b
                if e == 0:
                    pe.wait_ge(ctxT_lo_done, q * G + G)
                    pe.wait_ge(exp_lo_done, q * G + G)
                last = three_passes(banks(a, b)[j][:, :],
                                    (ctxT_hi[:, e, j * P:(j + 1) * P], ctxT_lo[:, e, j * P:(j + 1) * P]),
                                    (exp_hi[:, e, :], exp_lo[:, e, :]), e == 0, e == G - 1)
                if e == G - 1:
                    last.then_inc(mix_done, 1)

            def turn_xn2(a):
                pe.wait_ge(xn2_done, a * RT + RT)
                if later(a * HALF_SUMS):
                    pe.wait_ge(even_scaled, a * HALF_SUMS)
                if later(a * HALF_SUMS):
                    pe.wait_ge(odd_scaled, a * HALF_SUMS)
                for k in range(G):
                    for rt in range(RT):
                        last = nc.tensor.transpose(turn_banks[k][:, rt * P:(rt + 1) * P],
                                                   ctx_sb[rt // J][:, rt % J, k * P:(k + 1) * P], ident32[:, :])
                    last.then_inc(xn2_turned, 1)

            def group_sum(m, t, n):
                k, g = n // G, n % G
                done = m * HALF_SUMS + (t * 8 + n) // 2
                if later(done):
                    pe.wait_ge(even_scaled if n % 2 == 0 else odd_scaled, done)
                if t == 0 and k == 0:
                    pe.wait_ge(xT_lo_done, m * G + g + 1)
                if is_first(m) and t == 0 and n == 0:
                    pe.wait_ge(gu_copied, 2 * T)
                w = gateupT[:, g, k, t * P:(t + 1) * P]
                nc.tensor.matmul(psG[n % 2][:, :], w, xT_hi[:, g, :], start=True, stop=False)
                nc.tensor.matmul(psG[n % 2][:, :], w, xT_lo[:, g, :], start=False, stop=True).then_inc(group_sums, 1)

            def down(m, t, rt):
                if rt == 0:
                    pe.wait_ge(h_lo_done, m * T + t + 1)
                if t == 0:
                    if later(m * RT - RT + rt + 1):
                        pe.wait_ge(final_done, m * RT - RT + rt + 1)
                if is_first(m) and t == 0 and rt == 0:
                    pe.wait_ge(down_lo_done, T)
                cols = slice(rt * P, (rt + 1) * P)
                three_passes(psD[rt][:, :], (h_hi[:, t % HBUF, cols], h_lo[:, t % HBUF, cols]),
                             (down_hi[:, t, :], down_lo[:, t, :]), t == 0, t == T - 1).then_inc(down_done, 1)

            def turn_weights(c):
                pe.wait_ge(reordered, c + 1)
                if c == 0:
                    pe.wait_ge(scales_ready, 2)
                if c < len(GU_CHUNKS):
                    t0, t1 = GU_CHUNKS[c]
                    for i in range(2 * (t1 - t0)):
                        use = 2 * t0 + i
                        if later(use - RT + 1):
                            pe.wait_ge(gu_copied, use - RT + 1)
                        for g in range(G):
                            last = nc.tensor.matmul(psD[use % RT][:, g * P:(g + 1) * P],
                                                    values[:, i * D + g * P:i * D + (g + 1) * P], ident16[:, :],
                                                    start=True, stop=True)
                        last.then_inc(weights_turned, 1)
                else:
                    g0, g1 = DN_CHUNKS[c - len(GU_CHUNKS)]
                    pe.wait_ge(diag_made, c - len(GU_CHUNKS) + 1)
                    for g in range(g0, g1):
                        use = 2 * T + g
                        if use - RT < 2 * T:
                            pe.wait_ge(gu_copied, use - RT + 1)
                        else:
                            pe.wait_ge(down_lo_done, g - RT + 1)
                        for o in range(G):
                            at = (o * (g1 - g0) + g - g0) * P
                            last = nc.tensor.matmul(psD[use % RT][:, o * P:(o + 1) * P], values[:, at:at + P],
                                                    diag[:, o, g - g0, :], start=True, stop=True)
                        last.then_inc(weights_turned, 1)

            def attention(a, t, n):
                if (t, n) == (1, 7):
                    scores(a, 0, 0)
                elif (t, n) == (2, 2):
                    scores(a, 0, 1)
                elif (t, n) == (2, 4):
                    scores(a, 0, 2)
                elif (t, n) == (3, 1):
                    scores(a, 0, 3)
                elif (t, n) == (3, 4):
                    turn_ctx(a, 0, 0)
                elif (t, n) == (4, 2):
                    turn_ctx(a, 0, 1)
                elif (t, n) == (4, 6):
                    mix(a, 0, 0, 0)
                    mix(a, 0, 0, 1)
                elif (t, n) == (4, 7):
                    mix(a, 0, 0, 2)
                elif (t, n) == (5, 2):
                    mix(a, 0, 0, 3)
                elif (t, n) == (5, 4):
                    mix(a, 0, 1, 0)
                    mix(a, 0, 1, 1)
                elif (t, n) == (5, 6):
                    mix(a, 0, 1, 2)
                elif (t, n) == (6, 2):
                    mix(a, 0, 1, 3)
                elif (t, n) == (6, 4):
                    scores(a, 1, 0)
                elif (t, n) == (6, 6):
                    scores(a, 1, 1)
                elif (t, n) == (7, 2):
                    scores(a, 1, 2)
                elif (t, n) == (7, 4):
                    scores(a, 1, 3)
                elif (t, n) == (8, 1):
                    turn_ctx(a, 1, 0)
                elif (t, n) == (8, 3):
                    turn_ctx(a, 1, 1)
                elif (t, n) == (9, 0):
                    mix(a, 1, 0, 0)
                elif (t, n) == (9, 1):
                    mix(a, 1, 0, 1)
                elif (t, n) == (9, 3):
                    mix(a, 1, 0, 2)
                    mix(a, 1, 0, 3)
                elif (t, n) == (9, 4):
                    mix(a, 1, 1, 0)
                    mix(a, 1, 1, 1)
                elif (t, n) == (9, 6):
                    mix(a, 1, 1, 2)
                elif (t, n) == (9, 7):
                    mix(a, 1, 1, 3)

            def ffn(m, attend):
                for t in range(T):
                    for n in range(2 * G):
                        group_sum(m, t, n)
                        if t == 0 and n % 2 and not is_first(m):
                            down(m - 1, T - 2, n // 2)
                        if t == 1 and n < RT and not is_first(m):
                            down(m - 1, T - 1, n)
                        if t == 2 and n >= RT:
                            down(m, 0, n - RT)
                        if t > 2 and n % 2:
                            down(m, t - 2, n // 2)
                        if attend:
                            attention(m + 1, t, n)
                if attend:
                    turn_xn2(m + 1)

            pe.wait_ge(scales_in, 32)
            pe.wait_ge(ident_made, 4)
            nc.tensor.matmul(psD[0][:, 0:G * 2 * T], gu_scale_rows[:, :], ident16[0:G * 2 * T, 0:G * 2 * T],
                             start=True, stop=True).then_inc(scales_turned, 1)
            for o in range(G):
                last = nc.tensor.matmul(psD[1][:, o * T:(o + 1) * T], dn_scale_rows[:, o * P:(o + 1) * P],
                                        ident16[0:T, 0:T], start=True, stop=True)
            last.then_inc(scales_turned, 1)
            for e in range(4):
                scores(0, 0, e)
            turn_ctx(0, 0, 0)
            turn_ctx(0, 0, 1)
            turn_weights(0)
            for e in range(4):
                mix(0, 0, 0, e)
            for e in range(4):
                mix(0, 0, 1, e)
            turn_weights(1)
            for e in range(4):
                scores(0, 1, e)
            turn_ctx(0, 1, 0)
            turn_ctx(0, 1, 1)
            turn_weights(2)
            for e in range(4):
                mix(0, 1, 0, e)
            for e in range(4):
                mix(0, 1, 1, e)
            for e in range(3, 6):
                turn_weights(e)
            turn_xn2(0)
            ffn(0, True)
            with pe.Fori(1, MACROS - 1) as m:
                ffn(m, True)
            ffn(MACROS - 1, False)
            for t in (T - 2, T - 1):
                for rt in range(RT):
                    down(MACROS - 1, t, rt)

        @block.vector
        def _(dve):
            def layer_norm_stats(src, mean_var, var, stats, names, q, scale):
                stats_sem, aggr_sem, var_sem = names
                for j in range(J):
                    nc.vector.bn_stats(stats[:, j, :], src(j)).then_inc(stats_sem, 1)
                dve.wait_ge(stats_sem, q * J + J)
                nc.vector.memset(var, 0.0)
                for j in range(J):
                    nc.vector.bn_aggr(mean_var[:, j, :], stats[:, j, :]).then_inc(aggr_sem, 1)
                dve.wait_ge(aggr_sem, q * J + J)
                nc.vector.tensor_scalar(var, mean_var[:, :, 1], LN_EPS, scale, ALU.add, ALU.mult).then_inc(var_sem, 1)

            def ln1(a, b):
                dve.wait_ge(x_in[b], a * 16 + 16)
                layer_norm_stats(lambda j: x_sb[b][:, j, :], mv1[:, J * b:J * b + J, :], var1[:, J * b:J * b + J],
                                 bn[:, 0, J * b:J * b + J, :], (ln1_stats, ln1_aggr, ln1_var), a * 2 + b, float(D))

            def normalise1(a, b, j):
                q = a * 2 + b
                dve.wait_ge(rstd1_done, q + 1)
                if later(q * G):
                    dve.wait_ge(exp_lo_done, q * G)
                nc.vector.tensor_scalar(work[:, j, :], x_sb[b][:, j, :], mv1[:, J * b + j, 0:1],
                                        rstd1[:, J * b + j:J * b + j + 1],
                                        ALU.subtract, ALU.mult).then_inc(xn_done, 1)

            def maximum(a, b, e):
                q = a * 2 + b
                dve.wait_ge(scores_done, q * G + e + 1)
                nc.vector.tensor_reduce(neg_max[:, e:e + 1], banks(a, b)[e % 2][:, :], AXIS_X, ALU.max,
                                        negate=True).then_inc(max_done, 1)

            def inverse_sums(a, b):
                q = a * 2 + b
                dve.wait_ge(exp_done, q * G + G)
                nc.vector.reciprocal(inv_sum[:, :], exp_sum[:, :]).then_inc(inv_sum_done, 1)

            def split_ctxT(a, b, pair):
                q = a * 2 + b
                dve.wait_ge(ctx_turned, q * 2 + pair + 1)
                if pair == 0:
                    dve.wait_ge(inv_sum_done, q + 1)
                    if later(q * J):
                        dve.wait_ge(mix_done, q * J)
                for k in range(2):
                    e = 2 * pair + k
                    nc.vector.tensor_scalar(ctxT_hi[:, e, :], banks(a, b)[pair][:, k * 256:(k + 1) * 256],
                                            inv_sum[:, e:e + 1], None, ALU.mult).then_inc(ctxT_hi_done, 1)
                for k in range(2):
                    e = 2 * pair + k
                    dve.wait_ge(ctxT_hi_done, q * G + e + 1)
                    nc.vector.scalar_tensor_tensor(out=ctxT_lo[:, e, :], in0=banks(a, b)[pair][:, k * 256:(k + 1) * 256],
                                                   scalar=inv_sum[:, e:e + 1], in1=ctxT_hi[:, e, :].bitcast(F32),
                                                   op0=ALU.mult, op1=ALU.subtract).then_inc(ctxT_lo_done, 1)

            def residual(a, b, j):
                q = a * 2 + b
                dve.wait_ge(mix_done, q * J + j + 1)
                if later(a * 16):
                    dve.wait_ge(x2_copied, a * 16)
                nc.vector.tensor_tensor(x2_new[:, J * b + j, :], banks(a, b)[j][:, :], x_sb[b][:, j, :],
                                        ALU.add).then_inc(x2_done, 1)

            def ln2(a, b):
                q = a * 2 + b
                dve.wait_ge(x2_done, q * J + J)
                layer_norm_stats(lambda j: x2_new[:, J * b + j, :], mv2[:, J * b:J * b + J, :],
                                 var2[:, J * b:J * b + J], bn[:, 1, J * b:J * b + J, :],
                                 (ln2_stats, ln2_aggr, ln2_var), q, 1.0)

            def normalise2(a, b, j):
                q = a * 2 + b
                dve.wait_ge(rstd2_done, q + 1)
                rt = J * b + j
                nc.vector.tensor_scalar(ctx_sb[b][:, j, :], x2_new[:, rt, :], mv2[:, rt, 0:1],
                                        rstd2[:, rt:rt + 1], ALU.subtract, ALU.mult).then_inc(xn2_done, 1)

            def split_xT(a):
                for k in range(G):
                    dve.wait_ge(xT_hi_done, a * G + k + 1)
                    nc.vector.tensor_tensor(xT_lo[:, k, :], turn_banks[k][:, :], xT_hi[:, k, :].bitcast(F32),
                                            ALU.subtract).then_inc(xT_lo_done, 1)

            def scale_odd(m, t, n):
                k, g = n // G, n % G
                half = m * HALF_SUMS + (t * 8 + n) // 2
                dve.wait_ge(group_sums, m * GROUP_SUMS + t * 8 + n + 1)
                dve.wait_ge(even_scaled, half + 1)
                part = (part_a if g == 1 else part_b)[:, k, :]
                nc.vector.scalar_tensor_tensor(out=part, in0=psG[1][:, :], scalar=gu_scale[:, g, k, t:t + 1],
                                               in1=part, op0=ALU.mult, op1=ALU.add).then_inc(odd_scaled, 1)

            def silu(m, t):
                dve.wait_ge(tanh_done, m * T + t + 1)
                if later(m * T + t):
                    dve.wait_ge(h_lo_done, m * T + t)
                nc.vector.scalar_tensor_tensor(out=h[:, :], in0=tanh_g[:, :], scalar=1.0, in1=gate_up[:, 0, :],
                                               op0=ALU.add, op1=ALU.mult).then_inc(silu_done, 1)

            def times_up(m, t):
                dve.wait_ge(gate_up_done, m * (2 * T) + 2 * t + 2)
                dve.wait_ge(silu_done, m * T + t + 1)
                nc.vector.tensor_tensor(h[:, :], h[:, :], gate_up[:, 1, :], ALU.mult).then_inc(h_done, 1)

            def mean_squares(m):
                dve.wait_ge(squares_done, m * RT + RT)
                nc.vector.tensor_scalar(mean_sq[:, :], sq_sum[:, :], 1.0 / D, RMS_EPS, ALU.mult,
                                        ALU.add).then_inc(mean_sq_done, 1)

            def finish(m, rt):
                dve.wait_ge(inv_rms_done, m + 1)
                dve.wait_ge(x2_copied, m * 16 + 16)
                nc.vector.scalar_tensor_tensor(out=x2_cur[:, rt, :], in0=psD[rt][:, :], scalar=inv_rms[:, rt:rt + 1],
                                               in1=x2_cur[:, rt, :], op0=ALU.mult, op1=ALU.add).then_inc(final_done, 1)

            def decode(c, i):
                words, a, n = gu_chunk(c) if c < len(GU_CHUNKS) else dn_chunk(c - len(GU_CHUNKS))
                dve.wait_ge(gu_words_in if c < len(GU_CHUNKS) else dn_words_in, 16)
                if later(c):
                    dve.wait_ge(reordered, c)

                def view(t):
                    return t[:, 0:a * n].rearrange("p (a n) -> p a n", a=a)

                if later(4 * c + i):
                    dve.wait_ge(decoded, 4 * c + i)
                nc.vector.tensor_scalar(view(sign_bits), words, 12 - 4 * i, 0x80008000,
                                        ALU.logical_shift_left, ALU.bitwise_and).then_inc(bits_masked, 1)
                shift = ALU.logical_shift_left if i < 3 else ALU.logical_shift_right
                nc.vector.tensor_scalar(view(value_bits), words, abs(9 - 4 * i), 0x0E000E00,
                                        shift, ALU.bitwise_and).then_inc(bits_masked, 1)
                dve.wait_ge(bits_masked, 2 * (4 * c + i) + 2)
                nc.vector.tensor_tensor(planes[:, i, 0:a * n], sign_bits[:, 0:a * n], value_bits[:, 0:a * n],
                                        ALU.bitwise_or).then_inc(decoded, 1)

            def down_rest(c, k):
                g0, g1 = DN_CHUNKS[c]
                for g in range(g0 + 2 * k, min(g0 + 2 * k + 2, g1)):
                    use = 2 * T + g
                    dve.wait_ge(down_hi_done, g + 1)
                    nc.vector.scalar_tensor_tensor(out=down_lo[:, g, :], in0=psD[use % RT][:, :], scalar=16384.0,
                                                   in1=down_hi[:, g, :].bitcast(F32), op0=ALU.mult,
                                                   op1=ALU.subtract).then_inc(down_lo_done, 1)

            def gate_up_scales():
                dve.wait_ge(scales_turned, 1)
                turned = psD[0][:, 0:G * 2 * T].rearrange("p (g k t) -> p g k t", g=G, k=2)
                for k in range(2):
                    last = nc.vector.tensor_scalar(gu_scale[:, :, k, :], turned[:, :, k, :], 0.5 if k else 1.0, None,
                                                   ALU.mult)
                last.then_inc(scales_ready, 1)

            def down_scales():
                dve.wait_ge(scales_turned, 2)
                nc.vector.tensor_copy(dn_scale[:, :, :].rearrange("p o g -> p (o g)"),
                                      psD[1][:, 0:G * T]).then_inc(scales_ready, 1)

            def attention(a, t, n):
                if (t, n) == (0, 3):
                    ln1(a, 0)
                elif (t, n) == (0, 5):
                    normalise1(a, 0, 0)
                    normalise1(a, 0, 1)
                elif (t, n) == (1, 7):
                    maximum(a, 0, 0)
                elif (t, n) == (2, 3):
                    maximum(a, 0, 1)
                elif (t, n) == (2, 7):
                    maximum(a, 0, 2)
                elif (t, n) == (3, 1):
                    maximum(a, 0, 3)
                elif (t, n) == (3, 7):
                    inverse_sums(a, 0)
                elif (t, n) == (4, 1):
                    split_ctxT(a, 0, 0)
                elif (t, n) == (4, 3):
                    split_ctxT(a, 0, 1)
                elif (t, n) == (4, 5):
                    ln1(a, 1)
                elif (t, n) == (4, 7):
                    normalise1(a, 1, 0)
                    normalise1(a, 1, 1)
                elif (t, n) == (5, 7):
                    residual(a, 0, 0)
                elif (t, n) == (6, 1):
                    residual(a, 0, 1)
                elif (t, n) == (6, 3):
                    maximum(a, 1, 0)
                elif (t, n) == (6, 5):
                    ln2(a, 0)
                elif (t, n) == (6, 7):
                    maximum(a, 1, 1)
                elif (t, n) == (7, 1):
                    maximum(a, 1, 2)
                elif (t, n) == (7, 3):
                    maximum(a, 1, 3)
                elif (t, n) == (7, 5):
                    normalise2(a, 0, 0)
                    normalise2(a, 0, 1)
                elif (t, n) == (8, 1):
                    inverse_sums(a, 1)
                elif (t, n) == (8, 3):
                    split_ctxT(a, 1, 0)
                elif (t, n) == (8, 5):
                    split_ctxT(a, 1, 1)
                elif (t, n) == (9, 3):
                    residual(a, 1, 0)
                elif (t, n) == (9, 7):
                    residual(a, 1, 1)
                elif (t, n) == (10, 3):
                    ln2(a, 1)
                elif (t, n) == (10, 5):
                    normalise2(a, 1, 0)
                    normalise2(a, 1, 1)

            def output(m, t, n):
                if (t, n) == (1, 7):
                    mean_squares(m)
                elif (t, n) == (2, 1):
                    finish(m, 0)
                    finish(m, 1)
                elif (t, n) == (2, 3):
                    finish(m, 2)
                elif (t, n) == (2, 5):
                    finish(m, 3)

            def ffn(m, attend):
                first = is_first(m)
                for t in range(T):
                    for n in range(1, 2 * G, 2):
                        scale_odd(m, t, n)
                        if n == 1 and t > 0:
                            times_up(m, t - 1)
                        if n == 1 and t == 0 and not first:
                            times_up(m - 1, T - 1)
                        if n == 7:
                            silu(m, t)
                        if not first:
                            output(m - 1, t, n)
                        if attend:
                            attention(m + 1, t, n)
                if attend:
                    split_xT(m + 1)

            ln1(0, 0)
            normalise1(0, 0, 0)
            normalise1(0, 0, 1)
            for i in range(4):
                decode(0, i)
            gate_up_scales()
            ln1(0, 1)
            down_scales()
            maximum(0, 0, 0)
            maximum(0, 0, 1)
            decode(1, 0)
            maximum(0, 0, 2)
            decode(1, 1)
            maximum(0, 0, 3)
            decode(1, 2)
            inverse_sums(0, 0)
            split_ctxT(0, 0, 0)
            split_ctxT(0, 0, 1)
            normalise1(0, 1, 0)
            normalise1(0, 1, 1)
            decode(1, 3)
            residual(0, 0, 0)
            residual(0, 0, 1)
            ln2(0, 0)
            for i in range(4):
                decode(2, i)
            for e in range(4):
                maximum(0, 1, e)
            normalise2(0, 0, 0)
            normalise2(0, 0, 1)
            inverse_sums(0, 1)
            split_ctxT(0, 1, 0)
            split_ctxT(0, 1, 1)
            for i in range(4):
                decode(3, i)
            residual(0, 1, 0)
            residual(0, 1, 1)
            ln2(0, 1)
            normalise2(0, 1, 0)
            normalise2(0, 1, 1)
            for i in range(4):
                decode(4, i)
            down_rest(0, 0)
            down_rest(0, 1)
            for i in range(4):
                decode(5, i)
            down_rest(1, 0)
            down_rest(1, 1)
            split_xT(0)
            down_rest(2, 0)
            down_rest(2, 1)
            ffn(0, True)
            with dve.Fori(1, MACROS - 1) as m:
                ffn(m, True)
            ffn(MACROS - 1, False)
            times_up(MACROS - 1, T - 1)
            mean_squares(MACROS - 1)
            for rt in range(RT):
                finish(MACROS - 1, rt)

        @block.scalar
        def _(act):
            def xn_high(a, b, j):
                q = a * 2 + b
                if later(q * G):
                    act.wait_ge(scores_done, q * G)
                act.wait_ge(xn_done, q * J + j + 1)
                nc.scalar.activation(xn_hi[:, j, :], work[:, j, :], ACT.Copy).then_inc(xn_hi_done, 1)

            def ctx_high(a, b, j):
                q = a * 2 + b
                act.wait_ge(ctx_loaded[b], a * 16 + 16)
                if later(q * G):
                    act.wait_ge(scores_done, q * G)
                nc.scalar.activation(ctx_hi[:, j, :], ctx_sb[b][:, j, :], ACT.Copy).then_inc(ctx_hi_done, 1)

            def exponent(a, b, e):
                q = a * 2 + b
                act.wait_ge(max_done, q * G + e + 1)
                if later(q):
                    act.wait_ge(inv_sum_done, q)
                if e < 2:
                    act.wait_ge(xn_lo_done, q * J + J)
                else:
                    act.wait_ge(exp_lo_done, q * G + e - 1)
                nc.scalar.activation(work[:, e % 2, :], banks(a, b)[e % 2][:, :], ACT.Exp, bias=neg_max[:, e:e + 1],
                                     accum_out=exp_sum[:, e:e + 1]).then_inc(exp_done, 1)
                act.wait_ge(exp_done, q * G + e + 1)
                if later(q * J):
                    act.wait_ge(mix_done, q * J)
                nc.scalar.activation(exp_hi[:, e, :], work[:, e % 2, :], ACT.Copy).then_inc(exp_hi_done, 1)

            def xT_high(a):
                for k in range(G):
                    act.wait_ge(xn2_turned, a * G + k + 1)
                    nc.scalar.activation(xT_hi[:, k, :], turn_banks[k][:, :], ACT.Copy).then_inc(xT_hi_done, 1)

            def scale_even(m, t, n):
                k, g = n // G, n % G
                act.wait_ge(group_sums, m * GROUP_SUMS + t * 8 + n + 1)
                if later(m * (2 * T) + 2 * t + k - 1):
                    act.wait_ge(gate_up_done, m * (2 * T) + 2 * t + k - 1)
                part = (part_a if g == 0 else part_b)[:, k, :]
                nc.scalar.activation(part, psG[0][:, :], ACT.Copy, scale=gu_scale[:, g, k, t:t + 1]).then_inc(even_scaled, 1)

            def tanh(m, t):
                act.wait_ge(gate_up_done, m * (2 * T) + 2 * t + 1)
                if later(m * T + t):
                    act.wait_ge(silu_done, m * T + t)
                nc.scalar.activation(tanh_g[:, :], gate_up[:, 0, :], ACT.Tanh, scale=0.5).then_inc(tanh_done, 1)

            def h_high(m, t):
                act.wait_ge(h_done, m * T + t + 1)
                if later(down_users(m, t)):
                    act.wait_ge(down_done, down_users(m, t))
                nc.scalar.activation(h_hi[:, t % HBUF, :], h[:, :], ACT.Copy).then_inc(h_hi_done, 1)

            def squares(m, rt):
                act.wait_ge(down_done, m * (T * RT) + (T - 1) * RT + rt + 1)
                act.wait_ge(mean_sq_done, m)
                act.wait_ge(squares_done, m * RT + rt)
                nc.scalar.activation(square[:, :], psD[rt][:, :], ACT.Square,
                                     accum_out=sq_sum[:, rt:rt + 1]).then_inc(squares_done, 1)

            def reorder(c):
                n = (gu_chunk(c) if c < len(GU_CHUNKS) else dn_chunk(c - len(GU_CHUNKS)))
                n = n[1] * n[2]
                act.wait_ge(decoded, 4 * c + 4)
                if later(CHUNK_USES[c]):
                    act.wait_ge(weights_turned, CHUNK_USES[c])
                nc.scalar.activation(values[:, 0:8 * n].rearrange("p (q i) -> p i q", i=4),
                                     planes[:, :, 0:n].bitcast(F16), ACT.Copy).then_inc(reordered, 1)

            def copy_weights(c, k):
                if c < len(GU_CHUNKS):
                    t0, t1 = GU_CHUNKS[c]
                    for t in range(t0, t1):
                        use = 2 * t0 + k * (t1 - t0) + t - t0
                        act.wait_ge(weights_turned, use + 1)
                        nc.scalar.activation(gateupT[:, :, k, t * P:(t + 1) * P],
                                             psD[use % RT][:, :].rearrange("p (g o) -> p g o", g=G),
                                             ACT.Copy, scale=16384.0).then_inc(gu_copied, 1)
                else:
                    g0, g1 = DN_CHUNKS[c - len(GU_CHUNKS)]
                    for g in range(g0 + 2 * k, min(g0 + 2 * k + 2, g1)):
                        use = 2 * T + g
                        act.wait_ge(weights_turned, use + 1)
                        nc.scalar.activation(down_hi[:, g, :], psD[use % RT][:, :], ACT.Copy,
                                             scale=16384.0).then_inc(down_hi_done, 1)

            def attention(a, t, n):
                if (t, n) == (0, 4):
                    ctx_high(a, 0, 0)
                    ctx_high(a, 0, 1)
                elif (t, n) == (0, 6):
                    xn_high(a, 0, 0)
                    xn_high(a, 0, 1)
                elif (t, n) == (2, 2):
                    exponent(a, 0, 0)
                elif (t, n) == (2, 4):
                    exponent(a, 0, 1)
                elif (t, n) == (3, 0):
                    exponent(a, 0, 2)
                elif (t, n) == (3, 4):
                    exponent(a, 0, 3)
                elif (t, n) == (4, 2):
                    ctx_high(a, 1, 0)
                elif (t, n) == (5, 0):
                    ctx_high(a, 1, 1)
                    xn_high(a, 1, 0)
                elif (t, n) == (5, 4):
                    xn_high(a, 1, 1)
                elif (t, n) == (6, 6):
                    exponent(a, 1, 0)
                elif (t, n) == (7, 2):
                    exponent(a, 1, 1)
                elif (t, n) == (7, 4):
                    exponent(a, 1, 2)
                elif (t, n) == (8, 0):
                    exponent(a, 1, 3)

            def output(m, t, n):
                if (t, n) == (1, 0):
                    squares(m, 0)
                    squares(m, 1)
                elif (t, n) == (1, 4):
                    squares(m, 2)
                elif (t, n) == (1, 6):
                    squares(m, 3)

            def ffn(m, attend):
                first = is_first(m)
                for t in range(T):
                    for n in range(0, 2 * G, 2):
                        scale_even(m, t, n)
                        if n == 2 and t > 0:
                            h_high(m, t - 1)
                        if n == 2 and t == 0 and not first:
                            h_high(m - 1, T - 1)
                        if n == 6:
                            tanh(m, t)
                        if not first:
                            output(m - 1, t, n)
                        if attend:
                            attention(m + 1, t, n)
                if attend:
                    xT_high(m + 1)

            xn_high(0, 0, 0)
            xn_high(0, 0, 1)
            ctx_high(0, 0, 0)
            ctx_high(0, 0, 1)
            reorder(0)
            for e in range(4):
                exponent(0, 0, e)
            ctx_high(0, 1, 0)
            ctx_high(0, 1, 1)
            copy_weights(0, 0)
            copy_weights(0, 1)
            xn_high(0, 1, 0)
            xn_high(0, 1, 1)
            reorder(1)
            copy_weights(1, 0)
            copy_weights(1, 1)
            for e in range(4):
                exponent(0, 1, e)
            reorder(2)
            copy_weights(2, 0)
            copy_weights(2, 1)
            reorder(3)
            copy_weights(3, 0)
            copy_weights(3, 1)
            reorder(4)
            copy_weights(4, 0)
            copy_weights(4, 1)
            reorder(5)
            xT_high(0)
            copy_weights(5, 0)
            copy_weights(5, 1)
            ffn(0, True)
            with act.Fori(1, MACROS - 1) as m:
                ffn(m, True)
            ffn(MACROS - 1, False)
            h_high(MACROS - 1, T - 1)
            for rt in range(RT):
                squares(MACROS - 1, rt)

        @block.gpsimd
        def _(pool):
            def rstd_1(a, b):
                q = a * 2 + b
                pool.wait_ge(ln1_var, q + 1)
                nc.gpsimd.tensor_tensor(rstd1[:, J * b:J * b + J], var1[:, J * b:J * b + J], minus_half[:, 0:J],
                                        ALU.pow).then_inc(rstd1_done, 1)

            def rstd_2(a, b):
                q = a * 2 + b
                pool.wait_ge(ln2_var, q + 1)
                nc.gpsimd.tensor_tensor(rstd2[:, J * b:J * b + J], var2[:, J * b:J * b + J], minus_half[:, 0:J],
                                        ALU.pow).then_inc(rstd2_done, 1)

            def xn_low(a, b, j):
                q = a * 2 + b
                pool.wait_ge(xn_hi_done, q * J + j + 1)
                nc.gpsimd.tensor_tensor(xn_lo[:, j, :], work[:, j, :], xn_hi[:, j, :].bitcast(F32),
                                        ALU.subtract).then_inc(xn_lo_done, 1)

            def ctx_low(a, b, j):
                q = a * 2 + b
                pool.wait_ge(ctx_hi_done, q * J + j + 1)
                nc.gpsimd.tensor_tensor(ctx_lo[:, j, :], ctx_sb[b][:, j, :], ctx_hi[:, j, :].bitcast(F32),
                                        ALU.subtract).then_inc(ctx_lo_done, 1)

            def exp_low(a, b, e):
                q = a * 2 + b
                pool.wait_ge(exp_hi_done, q * G + e + 1)
                nc.gpsimd.tensor_tensor(exp_lo[:, e, :], work[:, e % 2, :], exp_hi[:, e, :].bitcast(F32),
                                        ALU.subtract).then_inc(exp_lo_done, 1)

            def add_parts(m, t, k):
                pool.wait_ge(odd_scaled, m * HALF_SUMS + t * G + 2 * k + 2)
                if k == 0:
                    if later(m * T + t):
                        pool.wait_ge(silu_done, m * T + t)
                else:
                    if later(m * T + t):
                        pool.wait_ge(h_done, m * T + t)
                nc.gpsimd.tensor_tensor(gate_up[:, k, :], part_a[:, k, :], part_b[:, k, :],
                                        ALU.add).then_inc(gate_up_done, 1)

            def h_low(m, t):
                pool.wait_ge(h_hi_done, m * T + t + 1)
                nc.gpsimd.tensor_tensor(h_lo[:, t % HBUF, :], h[:, :], h_hi[:, t % HBUF, :].bitcast(F32),
                                        ALU.subtract).then_inc(h_lo_done, 1)

            def inverse_rms(m):
                pool.wait_ge(mean_sq_done, m + 1)
                nc.gpsimd.tensor_tensor(inv_rms[:, :], mean_sq[:, :], minus_half[:, :], ALU.pow).then_inc(inv_rms_done, 1)

            def diagonals(c):
                g0, g1 = DN_CHUNKS[c]
                pool.wait_ge(scales_ready, 2)
                if later(CHUNK_USES[len(GU_CHUNKS) + c] if c else 0):
                    pool.wait_ge(weights_turned, CHUNK_USES[len(GU_CHUNKS) + c] if c else 0)
                for o in range(G):
                    last = nc.gpsimd.tensor_tensor(
                        diag[:, o, 0:g1 - g0, :], ident16[:, :].unsqueeze(1).broadcast_to([P, g1 - g0, P]),
                        dn_scale[:, o, g0:g1].unsqueeze(2).broadcast_to([P, g1 - g0, P]), ALU.mult)
                last.then_inc(diag_made, 1)

            def attention(a, t, n):
                if (t, n) == (0, 3):
                    rstd_1(a, 0)
                elif (t, n) == (0, 4):
                    ctx_low(a, 0, 0)
                elif (t, n) == (0, 5):
                    ctx_low(a, 0, 1)
                elif (t, n) == (1, 0):
                    xn_low(a, 0, 0)
                elif (t, n) == (1, 1):
                    xn_low(a, 0, 1)
                elif (t, n) == (2, 1):
                    exp_low(a, 0, 0)
                elif (t, n) == (3, 0):
                    exp_low(a, 0, 1)
                elif (t, n) == (3, 1):
                    exp_low(a, 0, 2)
                elif (t, n) == (3, 5):
                    exp_low(a, 0, 3)
                elif (t, n) == (4, 5):
                    rstd_1(a, 1)
                elif (t, n) == (4, 7):
                    ctx_low(a, 1, 0)
                    ctx_low(a, 1, 1)
                elif (t, n) == (5, 2):
                    xn_low(a, 1, 0)
                elif (t, n) == (5, 4):
                    xn_low(a, 1, 1)
                elif (t, n) == (6, 4):
                    rstd_2(a, 0)
                elif (t, n) == (7, 0):
                    exp_low(a, 1, 0)
                    exp_low(a, 1, 1)
                elif (t, n) == (7, 4):
                    exp_low(a, 1, 2)
                elif (t, n) == (7, 7):
                    exp_low(a, 1, 3)
                elif (t, n) == (10, 2):
                    rstd_2(a, 1)

            def output(m, t, n):
                if (t, n) == (2, 1):
                    inverse_rms(m)

            def ffn(m, attend):
                first = is_first(m)
                for t in range(T):
                    for n in range(2 * G):
                        if n == 2:
                            add_parts(m, t, 0)
                        if n == 4 and t > 0:
                            h_low(m, t - 1)
                        if n == 4 and t == 0 and not first:
                            h_low(m - 1, T - 1)
                        if n == 7:
                            add_parts(m, t, 1)
                        if not first:
                            output(m - 1, t, n)
                        if attend:
                            attention(m + 1, t, n)

            for ident in (ident32, ident16):
                made = 0 if ident is ident32 else 2
                nc.gpsimd.memset(ident[:, :], 0.0).then_inc(ident_made, 1)
                pool.wait_ge(ident_made, made + 1)
                nc.gpsimd.affine_select(out=ident[:, :], in_=ident[:, :], compare_op=ALU.not_equal, fill=1.0, base=0,
                                        pattern=[[-1, P]], channel_multiplier=1).then_inc(ident_made, 1)
            nc.gpsimd.memset(minus_half[:, :], -0.5).then_inc(ident_made, 1)
            pool.wait_ge(ident_made, 5)
            rstd_1(0, 0)
            xn_low(0, 0, 0)
            xn_low(0, 0, 1)
            ctx_low(0, 0, 0)
            ctx_low(0, 0, 1)
            rstd_1(0, 1)
            for e in range(4):
                exp_low(0, 0, e)
            xn_low(0, 1, 0)
            xn_low(0, 1, 1)
            ctx_low(0, 1, 0)
            ctx_low(0, 1, 1)
            diagonals(0)
            rstd_2(0, 0)
            for e in range(4):
                exp_low(0, 1, e)
            rstd_2(0, 1)
            diagonals(1)
            diagonals(2)
            ffn(0, True)
            with pool.Fori(1, MACROS - 1) as m:
                ffn(m, True)
            ffn(MACROS - 1, False)
            h_low(MACROS - 1, T - 1)
            inverse_rms(MACROS - 1)


_INS = ['x', 'ctx_2048', 'L0_ffn_gate_up_packed', 'L0_ffn_gate_up_scales', 'L0_ffn_down_packed', 'L0_ffn_down_scales']
_OUTS = [((16, 256, 512), 'float32')]


def kernel(**inputs):
    import numpy as _np
    import concourse.bacc as _bacc
    from concourse import mybir as _mybir
    from concourse.bass_utils import run_bass_kernel_spmd as _run

    nc = _bacc.Bacc("TRN2", target_bir_lowering=False, num_devices=1)
    arrays, args = {}, []
    for name in _INS:
        a = _np.ascontiguousarray(inputs[name])
        if a.dtype == _np.int32:
            a = a.view(_np.uint32)
        arrays[f"in_{name}_dram"] = a
        args.append(nc.dram_tensor(f"in_{name}_dram", a.shape, _mybir.dt.from_np(a.dtype), kind="ExternalInput").ap())
    for i, (shape, dtype) in enumerate(_OUTS):
        dt = _mybir.dt.from_np(_np.dtype(dtype))
        args.append(nc.dram_tensor(f"out_{i}_dram", shape, dt, kind="ExternalOutput").ap())
    xattn_ffn_kernel(nc, *args)
    r = _run(nc, [arrays], core_ids=[0])
    got = tuple(r.results[0][f"out_{i}_dram"] for i in range(len(_OUTS)))
    return got[0]
```
